# Optimizing a Trainium2 kernel written in Bass

```python
import numpy as np
import jax
import jax.numpy as jnp

def _softmax(x, axis=-1):
    return jax.nn.softmax(x, axis=axis)

def _gelu(x):
    return jax.nn.gelu(x, approximate=True)

def _silu(x):
    return jax.nn.silu(x)

def _sigmoid(x):
    return jax.nn.sigmoid(x)

def _layernorm(x, axis=-1, eps=1e-05):
    m = jnp.mean(x, axis=axis, keepdims=True)
    v = jnp.var(x, axis=axis, keepdims=True)
    return (x - m) / jnp.sqrt(v + eps)

def _scatter_add(tgt, idx, src, axis=0):
    return tgt.at[idx].add(src)

def _segment_sum(src, seg, n):
    return jax.ops.segment_sum(src, seg, n)
kernel_name = 'mk_gnn_preln_d1_gnn_r8_0c8c36'

def setup_inputs(seed: int=0):
    np.random.seed(seed)
    _w = jnp.asarray

    def _rec_inputs():
        import jax
        import jax.numpy as jnp
        _gk = jax.random.key(seed)
        x = -0.0005121 + 1.001 * jax.random.normal(jax.random.fold_in(_gk, 1), (12500, 64), jnp.float32)
        src = jax.random.randint(jax.random.fold_in(_gk, 2), (200000,), 0, 12500, jnp.int32)
        dst = jnp.minimum((12500 * jax.random.uniform(jax.random.fold_in(_gk, 3), (200000,)) ** 2.0).astype(jnp.int32), 99999)
        _o = jnp.argsort(dst, stable=True)
        src = src[_o]
        dst = dst[_o]
        edge_attr_64 = 0.000189758 + 1.00013 * jax.random.normal(jax.random.fold_in(_gk, 12), (200000, 64), jnp.float32)
        return (x, src, dst, edge_attr_64)
    x, src, dst, edge_attr_64 = _rec_inputs()

    def _L0_gnn_setup():
        import jax, jax.numpy as jnp
        import numpy as np
        N, E, H, G = (6250, 100000, 64, 256)
        HID = 64
        EPS = 1e-05

        def _mk_mlp(key, n_in, n_out, hid=HID):
            ks = jax.random.split(key, 8)

            def lin(k, i, o):
                s = 1.0 / np.sqrt(i)
                return (jax.random.uniform(k, (i, o), jnp.float32, -s, s), jnp.zeros((o,), jnp.float32))
            w0, b0 = lin(ks[0], n_in, hid)
            w1, b1 = lin(ks[1], hid, hid)
            w2, b2 = lin(ks[2], hid, hid)
            g = jnp.ones((hid,), jnp.float32)
            be = jnp.zeros((hid,), jnp.float32)
            wo, bo = lin(ks[3], hid, n_out)
            return (w0, b0, w1, b1, w2, b2, g, be, wo, bo)

        def _mlp(h, w0, b0, w1, b1, w2, b2, g, be, wo, bo):
            h = jax.nn.relu(h @ w0 + b0)
            h = jax.nn.relu(h @ w1 + b1)
            h = jax.nn.relu(h @ w2 + b2)
            mu = jnp.mean(h, axis=-1, keepdims=True)
            var = jnp.mean(jnp.square(h - mu), axis=-1, keepdims=True)
            h = (h - mu) / jnp.sqrt(var + EPS) * g + be
            return h @ wo + bo
        key = jax.random.key(seed)
        ks = jax.random.split(key, 8)
        d = {}
        d['x'] = jax.random.normal(ks[0], (N, H), jnp.float32)
        d['edge_index'] = jax.random.randint(ks[1], (2, E), 0, N, dtype=jnp.int32)
        d['edge_attr'] = jax.random.normal(ks[2], (E, H), jnp.float32)
        d['u'] = jax.random.normal(ks[3], (G, H), jnp.float32)
        d['batch'] = jnp.sort(jax.random.randint(ks[4], (N,), 0, G, dtype=jnp.int32))
        p1 = _mk_mlp(ks[5], 2 * H, H)
        p2 = _mk_mlp(ks[6], 3 * H, H)
        names1 = ['w1_0', 'b1_0', 'w1_1', 'b1_1', 'w1_2', 'b1_2', 'g1', 'be1', 'w1_o', 'b1_o']
        names2 = ['w2_0', 'b2_0', 'w2_1', 'b2_1', 'w2_2', 'b2_2', 'g2', 'be2', 'w2_o', 'b2_o']
        for n, v in zip(names1, p1):
            d[n] = v
        for n, v in zip(names2, p2):
            d[n] = v
        return d
    _L0_gnn_all = _L0_gnn_setup()
    _L0_gnn_in = {k: v for k, v in _L0_gnn_all.items() if k in ('u', 'w1_0', 'b1_0', 'w1_1', 'b1_1', 'w1_2', 'b1_2', 'g1', 'be1', 'w1_o', 'b1_o', 'w2_0', 'b2_0', 'w2_1', 'b2_1', 'w2_2', 'b2_2', 'g2', 'be2', 'w2_o', 'b2_o')}
    del _L0_gnn_all
    return {'x': x, 'src': src, 'dst': dst, 'edge_attr_64': edge_attr_64, 'L0_gnn_u': _L0_gnn_in['u'], 'L0_gnn_w1_0': _L0_gnn_in['w1_0'], 'L0_gnn_b1_0': _L0_gnn_in['b1_0'], 'L0_gnn_w1_1': _L0_gnn_in['w1_1'], 'L0_gnn_b1_1': _L0_gnn_in['b1_1'], 'L0_gnn_w1_2': _L0_gnn_in['w1_2'], 'L0_gnn_b1_2': _L0_gnn_in['b1_2'], 'L0_gnn_g1': _L0_gnn_in['g1'], 'L0_gnn_be1': _L0_gnn_in['be1'], 'L0_gnn_w1_o': _L0_gnn_in['w1_o'], 'L0_gnn_b1_o': _L0_gnn_in['b1_o'], 'L0_gnn_w2_0': _L0_gnn_in['w2_0'], 'L0_gnn_b2_0': _L0_gnn_in['b2_0'], 'L0_gnn_w2_1': _L0_gnn_in['w2_1'], 'L0_gnn_b2_1': _L0_gnn_in['b2_1'], 'L0_gnn_w2_2': _L0_gnn_in['w2_2'], 'L0_gnn_b2_2': _L0_gnn_in['b2_2'], 'L0_gnn_g2': _L0_gnn_in['g2'], 'L0_gnn_be2': _L0_gnn_in['be2'], 'L0_gnn_w2_o': _L0_gnn_in['w2_o'], 'L0_gnn_b2_o': _L0_gnn_in['b2_o']}

def reference(x, src, dst, edge_attr_64, L0_gnn_u, L0_gnn_w1_0, L0_gnn_b1_0, L0_gnn_w1_1, L0_gnn_b1_1, L0_gnn_w1_2, L0_gnn_b1_2, L0_gnn_g1, L0_gnn_be1, L0_gnn_w1_o, L0_gnn_b1_o, L0_gnn_w2_0, L0_gnn_b2_0, L0_gnn_w2_1, L0_gnn_b2_1, L0_gnn_w2_2, L0_gnn_b2_2, L0_gnn_g2, L0_gnn_be2, L0_gnn_w2_o, L0_gnn_b2_o):
    import jax
    import jax.numpy as jnp

    def _L0_gnn_ref(x, edge_index, edge_attr, u, batch, w1_0, b1_0, w1_1, b1_1, w1_2, b1_2, g1, be1, w1_o, b1_o, w2_0, b2_0, w2_1, b2_1, w2_2, b2_2, g2, be2, w2_o, b2_o):
        import jax, jax.numpy as jnp
        import numpy as np
        N, E, H, G = (6250, 100000, 64, 256)
        HID = 64
        EPS = 1e-05

        def _mk_mlp(key, n_in, n_out, hid=HID):
            ks = jax.random.split(key, 8)

            def lin(k, i, o):
                s = 1.0 / np.sqrt(i)
                return (jax.random.uniform(k, (i, o), jnp.float32, -s, s), jnp.zeros((o,), jnp.float32))
            w0, b0 = lin(ks[0], n_in, hid)
            w1, b1 = lin(ks[1], hid, hid)
            w2, b2 = lin(ks[2], hid, hid)
            g = jnp.ones((hid,), jnp.float32)
            be = jnp.zeros((hid,), jnp.float32)
            wo, bo = lin(ks[3], hid, n_out)
            return (w0, b0, w1, b1, w2, b2, g, be, wo, bo)

        def _mlp(h, w0, b0, w1, b1, w2, b2, g, be, wo, bo):
            h = jax.nn.relu(h @ w0 + b0)
            h = jax.nn.relu(h @ w1 + b1)
            h = jax.nn.relu(h @ w2 + b2)
            mu = jnp.mean(h, axis=-1, keepdims=True)
            var = jnp.mean(jnp.square(h - mu), axis=-1, keepdims=True)
            h = (h - mu) / jnp.sqrt(var + EPS) * g + be
            return h @ wo + bo
        row, col = (edge_index[0], edge_index[1])
        msg = jnp.concatenate([x[row], edge_attr], axis=1)
        msg = _mlp(msg, w1_0, b1_0, w1_1, b1_1, w1_2, b1_2, g1, be1, w1_o, b1_o)
        agg = jax.ops.segment_sum(msg, col, num_segments=x.shape[0])
        h = jnp.concatenate([x, agg, u[batch]], axis=1)
        return x + _mlp(h, w2_0, b2_0, w2_1, b2_1, w2_2, b2_2, g2, be2, w2_o, b2_o)
    edge_index = jnp.stack([src, dst])
    batch0 = jnp.zeros((12500,), jnp.int32)
    h = jnp.maximum(_layernorm(x, axis=-1), 0.0)
    x = x + _L0_gnn_ref(h, edge_index, edge_attr_64, L0_gnn_u, batch0, L0_gnn_w1_0, L0_gnn_b1_0, L0_gnn_w1_1, L0_gnn_b1_1, L0_gnn_w1_2, L0_gnn_b1_2, L0_gnn_g1, L0_gnn_be1, L0_gnn_w1_o, L0_gnn_b1_o, L0_gnn_w2_0, L0_gnn_b2_0, L0_gnn_w2_1, L0_gnn_b2_1, L0_gnn_w2_2, L0_gnn_b2_2, L0_gnn_g2, L0_gnn_be2, L0_gnn_w2_o, L0_gnn_b2_o)
    return x

_drawn_inputs = setup_inputs


def setup_inputs(seed=0):
    import zlib

    import numpy as np

    out = dict(_drawn_inputs(seed))
    spreads = {'L0_gnn_b1_0': (0.0, 0.1),
     'L0_gnn_b1_1': (0.0, 0.1),
     'L0_gnn_b1_2': (0.0, 0.1),
     'L0_gnn_g1': (1.0, 0.2),
     'L0_gnn_be1': (0.0, 0.1),
     'L0_gnn_b1_o': (0.0, 0.1),
     'L0_gnn_b2_0': (0.0, 0.367),
     'L0_gnn_b2_1': (0.0, 0.1),
     'L0_gnn_b2_2': (0.0, 0.1),
     'L0_gnn_g2': (1.0, 0.2),
     'L0_gnn_be2': (0.0, 0.1),
     'L0_gnn_b2_o': (0.0, 0.1)}
    factors = {}
    for name, (base, spread) in spreads.items():
        noise = np.random.default_rng([zlib.crc32(name.encode()), seed]).standard_normal(out[name].shape)
        drawn = base * np.exp(spread * noise) if base else spread * noise
        out[name] = jnp.asarray(drawn.astype(out[name].dtype))
    for name, factor in factors.items():
        out[name] = (out[name] * factor).astype(out[name].dtype)
    return out
```

```python
import concourse.bass as bass
from concourse import mybir
from contextlib import ExitStack


def gnn_layer(nc, x, src, dst, edge_attr, u,
              w1_0, b1_0, w1_1, b1_1, w1_2, b1_2, g1, be1, w1_o, b1_o,
              w2_0, b2_0, w2_1, b2_1, w2_2, b2_2, g2, be2, w2_o, b2_o, h_dram, out):
    f32, i32 = mybir.dt.float32, mybir.dt.int32
    ALU, ACT, AX = mybir.AluOpType, mybir.ActivationFunctionType, mybir.AxisListType

    P = 128
    N, H = x.shape
    E = src.shape[0]
    EPS = 1e-5
    TILES = 8
    HALF = TILES // 2
    GROUP = TILES * P
    CHUNK = 2 * P
    CPG = GROUP // CHUNK
    WIN = 64
    GROUPS = 2 * -(-E // (2 * GROUP))
    FULL = E // GROUP
    assert FULL == GROUPS - 1 and E % 2 == 0 and GROUPS >= 6
    CHUNKS = GROUPS * CPG
    CBLK = -(-CHUNKS // P)
    NODES = HALF * P
    NBLK = -(-N // NODES)
    LASTP = (N - (NBLK - 1) * NODES) // HALF
    assert (N - (NBLK - 1) * NODES) % HALF == 0
    NT = NBLK * HALF
    PIECE = 5
    PIECES = [(b, min(b + PIECE, NBLK)) for b in range(0, NBLK, PIECE)]
    PAIRS = -(-NBLK // 2)
    AGGW = 2 * PAIRS * NODES + WIN
    PAD = -float(1 << 22)
    SLOW = 64
    assert E % SLOW == 0

    REALC = -(-E // CHUNK)
    TAILC = REALC - FULL * CPG
    TABK = -(-CBLK // 2)
    TABS = 2 * TABK
    NATS = 2 * sum(1 for n in (E // (P * CHUNK), E % (P * CHUNK) // CHUNK, E % CHUNK) if n)
    XS = [(b1 - b0 > (b1 == NBLK)) + (b1 == NBLK) for b0, b1 in PIECES]
    HD = sum(XS)
    WS = 7 + 6 + 12 + 1 + 12
    WC = 4
    OUTS = [sum(16 * ((min(2 * q + 2, NBLK) - 2 * q > (2 * q + 2 >= NBLK)) + (2 * q + 2 >= NBLK))
                for q in range(PAIRS) if q % 2 == k) for k in range(2)]

    ctx = ExitStack()
    with ctx:
        def sb(name, shape, dt=f32):
            return ctx.enter_context(nc.sbuf_tensor(name, shape, dt))

        def sem(name):
            return ctx.enter_context(nc.semaphore(name))

        node_in = sb("node_in", [P, AGGW])
        xh = sb("xh", [P, 2, NT, H])
        nat = sb("nat", [P, 2, CBLK, CHUNK], i32)
        natf = sb("natf", [P, 2, CBLK, CHUNK])
        base_f = sb("base_f", [P, CBLK])
        src_tab = sb("src_tab", [P, CBLK * P, 2], i32)
        dst_tab = sb("dst_tab", [P, CBLK * P, 2])
        base_row = sb("base_row", [1, CHUNKS], i32)
        rows = sb("rows", [P, 2, 2, TILES, H])
        idx = sb("idx", [P, 2, TILES], i32)
        xT = sb("xT", [P, GROUP])
        h0 = sb("h0", [P, NODES])
        h1 = sb("h1", [P, NODES])
        h2 = sb("h2", [P, NODES])
        cen = sb("cen", [P, 2, TILES, H])
        onehot = sb("onehot", [P, 2, TILES, WIN])
        bn = sb("bn", [P, PIECE * HALF, 6])
        st = sb("st", [P, 8, PIECE * HALF])
        eps = sb("eps", [P, 1])
        ident = sb("ident", [P, P])
        iota = sb("iota", [P, WIN])
        ones = sb("ones", [P, 1])
        one_row = sb("one_row", [1, P])
        bad = sb("bad", [P, 1])
        flag = sb("flag", [1, 1], i32)
        wl0 = sb("wl0", [P, H])
        wl0h = sb("wl0h", [P, P])
        wl0e = sb("wl0e", [P, P])
        wl1 = sb("wl1", [P, P])
        wl2 = sb("wl2", [P, P])
        bias1 = sb("bias1", [P, 3])
        wn0 = sb("wn0", [P, H])
        wn1 = sb("wn1", [P, P])
        wn2 = sb("wn2", [P, P])
        wno = sb("wno", [P, P])
        bias2 = sb("bias2", [P, 3])
        w1o_s = sb("w1o_s", [H, H])
        w2a_s = sb("w2a_s", [H, H])
        w2u_s = sb("w2u_s", [H, H])
        w2o_s = sb("w2o_s", [H, H])
        col = sb("col", [H, 6])
        drop63 = sb("drop63", [H, H])
        lnw = sb("lnw", [H, 3, H])
        bo_row = sb("bo_row", [1, H])
        bo_all = sb("bo_all", [P, H])
        res = sb("res", [P, 2, 2 * HALF, H])
        slow_rows = sb("slow_rows", [SLOW, 2, H])
        slow_idx = sb("slow_idx", [SLOW, 1], i32)
        slow_dst = sb("slow_dst", [1, SLOW], i32)
        slow_cen = sb("slow_cen", [SLOW, H])
        slow_diag = sb("slow_diag", [SLOW, SLOW])
        slow_msg = sb("slow_msg", [H, SLOW])

        def bank(name):
            return ctx.enter_context(nc.psum_tensor(name, [P, 512], f32))

        ps_ta, ps_tb, ps_l0, ps_l1, ps_l2, ps_t2 = (bank(n) for n in ("ta", "tb", "l0", "l1", "l2", "t2"))
        ps_agg = [bank("agg0"), bank("agg1")]
        ps_tab = [ps_ta, ps_tb, ps_l0, ps_l1]

        s_x = [sem(f"s_x{i}") for i in range(len(PIECES))]
        s_natm = sem("s_natm")
        s_nat = sem("s_nat")
        s_w = sem("s_w")
        s_wz = sem("s_wz")
        s_const = sem("s_const")
        s_pool = sem("s_pool")
        s_natf = sem("s_natf")
        s_marked = sem("s_marked")
        s_bad = sem("s_bad")
        s_ln = sem("s_ln")
        s_lvar, s_lroot = sem("s_lvar"), sem("s_lroot")
        s_var, s_root = sem("s_var"), sem("s_root")
        s_nvar, s_nroot = sem("s_nvar"), sem("s_nroot")
        s_fvar, s_froot = sem("s_fvar"), sem("s_froot")
        s_hd = sem("s_hd")
        s_tabp = sem("s_tabp")
        s_tabc = sem("s_tabc")
        s_hT = sem("s_hT")
        s_hTc = sem("s_hTc")
        s_wp = sem("s_wp")
        s_wc = sem("s_wc")
        s_flagp = sem("s_flagp")
        s_flag = sem("s_flag")
        s_idx = [sem("s_idx0"), sem("s_idx1")]
        s_gath = [sem("s_gath0"), sem("s_gath1")]
        s_attr = [sem("s_attr0"), sem("s_attr1")]
        s_tra, s_trb = sem("s_tra"), sem("s_trb")
        s_xa, s_xb = sem("s_xa"), sem("s_xb")
        s_l0, s_l1, s_l2 = sem("s_l0"), sem("s_l1"), sem("s_l2")
        s_h0, s_h1, s_h2 = sem("s_h0"), sem("s_h1"), sem("s_h2")
        s_t2 = sem("s_t2")
        s_rd = sem("s_rd")
        s_cen = sem("s_cen")
        s_oh = sem("s_oh")
        s_agg = sem("s_agg")
        s_add = sem("s_add")
        s_dve = sem("s_dve")
        s_st = sem("s_st")
        s_zero = sem("s_zero")
        s_fz, s_fload, s_fin, s_fg, s_frow, s_fT, s_fx, s_fU, s_fs, s_frd, s_fm, s_fc, s_fadd, s_fd = (
            sem("s_f_" + n) for n in ("zero", "load", "in", "gath", "row", "T", "x", "U", "chain", "rd", "m",
                                      "c", "add", "done"))
        s_fl, s_fh = [sem(f"s_fl{k}") for k in range(3)], [sem(f"s_fh{k}") for k in range(3)]
        s_sums = sem("s_sums")
        s_n0, s_n1, s_n2, s_nt, s_no = (sem(f"s_n{k}") for k in "012to")
        s_nh0, s_nh1, s_nh2 = (sem(f"s_nh{k}") for k in "012")
        s_nst, s_nread, s_nres, s_xs, s_xs1 = (sem(n) for n in ("s_nst", "s_nread", "s_nres", "s_xs", "s_xs1"))
        s_out = [sem("s_out0"), sem("s_out1")]

        def attr_rows(e0, chunks, parts):
            return edge_attr[bass.ds(e0, (chunks - 1) * CHUNK + 2 * parts), :].rearrange(
                "(c p t) d -> p c (t d)", c=chunks, t=2)

        def node_rows(t, b0, b1):
            return t[b0 * NODES:b1 * NODES, :].rearrange("(b p t) d -> p b (t d)", p=P, t=HALF)

        def node_tail(t):
            return t[(NBLK - 1) * NODES:N, :].rearrange("(p t) d -> p (t d)", t=HALF)

        block = ctx.enter_context(nc.Block())

        def mean_steps(link, parts, tiles):
            b = bn[0:parts, 0:tiles, :]
            s = st[0:parts, :, 0:tiles]
            link(nc.vector.tensor_tensor(s[:, 0, :], b[:, :, 1], b[:, :, 4], ALU.subtract))
            nc.vector.scalar_tensor_tensor(s[:, 2, :], s[:, 0, :], 0.25, s[:, 0, :], ALU.mult, ALU.mult)
            nc.vector.tensor_tensor(s[:, 3, :], b[:, :, 2], b[:, :, 5], ALU.add)
            link(nc.vector.scalar_tensor_tensor(s[:, 1, :], s[:, 0, :], -0.5, b[:, :, 1], ALU.mult, ALU.add))

        def var_step(parts, tiles):
            s = st[0:parts, :, 0:tiles]
            return nc.vector.scalar_tensor_tensor(s[:, 4, :], s[:, 3, :], 1.0 / H, s[:, 2, :], ALU.mult, ALU.add)

        def root_step(parts, tiles):
            return nc.scalar.activation(st[0:parts, 6, 0:tiles], st[0:parts, 4, 0:tiles], ACT.Sqrt, bias=eps[0:parts, :])

        def rstd_steps(link, parts, tiles):
            s = st[0:parts, :, 0:tiles]
            link(nc.vector.reciprocal(s[:, 6, :], s[:, 6, :]))
            link(nc.vector.tensor_tensor(s[:, 7, :], s[:, 6, :], s[:, 6, :], ALU.mult))
            link(nc.vector.scalar_tensor_tensor(s[:, 7, :], s[:, 4, :], EPS, s[:, 7, :], ALU.add, ALU.mult))
            link(nc.vector.tensor_scalar(s[:, 7, :], s[:, 7, :], -0.5, 1.5, ALU.mult, ALU.add))
            link(nc.vector.tensor_tensor(s[:, 5, :], s[:, 6, :], s[:, 7, :], ALU.mult))

        @block.sync
        def _(sp):
            sp.wait_ge(s_natm, 2)
            full = E // (P * CHUNK)
            rest = (E - full * P * CHUNK) // CHUNK
            left = E - (full * P + rest) * CHUNK
            for k, a in enumerate((src, dst)):
                if full:
                    sp.dma_start(nat[:, k, 0:full, :],
                                 a[0:full * P * CHUNK].rearrange("(b p e) -> p b e", p=P, e=CHUNK)).then_inc(s_nat, 16)
                if rest:
                    sp.dma_start(nat[0:rest, k, full, :],
                                 a[full * P * CHUNK:(full * P + rest) * CHUNK].rearrange("(p e) -> p e", e=CHUNK)
                                 ).then_inc(s_nat, 16)
                if left:
                    sp.dma_start(nat[rest:rest + 1, k, full, 0:left],
                                 a[E - left:E].rearrange("(p e) -> p e", p=1)).then_inc(s_nat, 16)
            for i, (b0, b1) in enumerate(PIECES):
                last = b1 == NBLK
                fb = b1 - 1 if last else b1
                if last:
                    sp.wait_ge(s_zero, 2)
                if fb > b0:
                    sp.dma_start(xh[:, 0, b0 * HALF:fb * HALF, :].rearrange("p (b t) d -> p b (t d)", t=HALF),
                                 node_rows(x, b0, fb)).then_inc(s_x[i], 16)
                if last:
                    sp.dma_start(xh[0:LASTP, 0, (NBLK - 1) * HALF:NT, :].rearrange("p t d -> p (t d)"),
                                 node_tail(x)).then_inc(s_x[i], 16)
            for g in range(2):
                sp.dma_start(rows[:, g, 1, :, :].rearrange("p (c t) d -> p c (t d)", t=2),
                             attr_rows(g * GROUP, CPG, P)).then_inc(s_attr[g], 16)
            for i, (b0, b1) in enumerate(PIECES):
                last = b1 == NBLK
                fb = b1 - 1 if last else b1
                sp.wait_ge(s_ln, i + 1)
                if fb > b0:
                    sp.dma_start(node_rows(h_dram, b0, fb),
                                 xh[:, 1, b0 * HALF:fb * HALF, :].rearrange("p (b t) d -> p b (t d)", t=HALF)
                                 ).then_inc(s_hd, 16)
                if last:
                    sp.dma_start(node_tail(h_dram),
                                 xh[0:LASTP, 1, (NBLK - 1) * HALF:NT, :].rearrange("p t d -> p (t d)")
                                 ).then_inc(s_hd, 16)

            with sp.Fori(2, GROUPS - 2, 2) as g:
                for k in range(2):
                    sp.wait_ge(s_trb, g + k - 1)
                    sp.dma_start(rows[:, k, 1, :, :].rearrange("p (c t) d -> p c (t d)", t=2),
                                 attr_rows(g * GROUP + k * GROUP, CPG, P)).then_inc(s_attr[k], 16)
            g = GROUPS - 2
            sp.wait_ge(s_trb, g - 1)
            sp.dma_start(rows[:, 0, 1, :, :].rearrange("p (c t) d -> p c (t d)", t=2),
                         attr_rows(g * GROUP, CPG, P)).then_inc(s_attr[0], 16)
            g = GROUPS - 1
            sp.wait_ge(s_trb, g - 1)
            for c in range(TAILC):
                n = min(CHUNK, E - g * GROUP - c * CHUNK) // 2
                sp.dma_start(rows[0:n, 1, 1, 2 * c:2 * c + 2, :].rearrange("p t d -> p (t d)"),
                             attr_rows(g * GROUP + c * CHUNK, 1, n).rearrange("p c d -> p (c d)")).then_inc(s_attr[1], 16)

            sp.wait_ge(s_flag, 1)
            f = sp.value_load(flag[0:1, 0:1], min_val=0, max_val=P)
            with sp.If(f > 0):
                with sp.Fori(1, E // SLOW + 1) as v:
                    sp.wait_ge(s_fd, v)
                    e0 = v * SLOW - SLOW
                    sp.dma_start(slow_idx[:, :], src[bass.ds(e0, SLOW)].rearrange("(p o) -> p o", o=1)).then_inc(s_fload, 16)
                    sp.dma_start(slow_dst[:, :], dst[bass.ds(e0, SLOW)].rearrange("(o e) -> o e", o=1)).then_inc(s_fload, 16)
                    sp.dma_start(slow_rows[:, 1, :], edge_attr[bass.ds(e0, SLOW), :]).then_inc(s_fload, 16)
                    sp.wait_ge(s_fload, v * 48)
                    sp.sem_inc(s_fin, 1)

            for q in range(PAIRS):
                sp.wait_ge(s_nres, q + 1)
                b0, b1 = 2 * q, min(2 * q + 2, NBLK)
                fb = b1 - 1 if b1 == NBLK else b1
                if fb > b0:
                    sp.dma_start(node_rows(out, b0, fb),
                                 res[:, q % 2, 0:(fb - b0) * HALF, :].rearrange("p (b t) d -> p b (t d)", t=HALF)
                                 ).then_inc(s_out[q % 2], 16)
                if b1 == NBLK:
                    sp.dma_start(node_tail(out), res[0:LASTP, q % 2, (fb - b0) * HALF:(fb - b0 + 1) * HALF, :]
                                 .rearrange("p t d -> p (t d)")).then_inc(s_out[q % 2], 16)
            for k in range(2):
                sp.wait_ge(s_out[k], OUTS[k])
            sp.wait_ge(s_hd, 16 * HD)

        @block.gpsimd
        def _(pool):
            pool.memset(nat[:, 0, CBLK - 1, :], 0).then_inc(s_natm, 1)
            pool.memset(nat[:, 1, CBLK - 1, :], int(PAD)).then_inc(s_natm, 1)
            for w in (wl0h, wl0e, wl1, wl2, wn1, wn2, wno):
                pool.memset(w[:, :], 0.0).then_inc(s_wz, 1)
            pool.memset(ident[:, :], 0.0)
            pool.memset(drop63[:, :], 0.0)
            pool.memset(ones[:, :], 1.0)
            pool.memset(eps[:, :], EPS)
            pool.memset(one_row[:, :], 1.0)
            pool.memset(lnw[:, 2, :], -1.0 / H)
            pool.iota(iota[:, :], pattern=[[1, WIN]], base=0, channel_multiplier=0,
                      allow_small_or_imprecise_dtypes=True).then_inc(s_pool, 1)
            pool.wait_ge(s_pool, 1)
            pool.affine_select(out=ident[:, :], in_=ident[:, :], compare_op=ALU.not_equal, fill=1.0,
                               base=0, pattern=[[-1, P]], channel_multiplier=1)
            pool.affine_select(out=drop63[:, :], in_=drop63[:, :], compare_op=ALU.not_equal, fill=-1.0,
                               base=1 - H, pattern=[[0, H]], channel_multiplier=1).then_inc(s_pool, 1)
            pool.wait_ge(s_pool, 2)
            pool.affine_select(out=drop63[:, :], in_=drop63[:, :], compare_op=ALU.not_equal, fill=1.0,
                               base=0, pattern=[[-1, H]], channel_multiplier=1)
            pool.tensor_tensor(lnw[:, 2, :], lnw[:, 2, :], ident[0:H, 0:H], ALU.add).then_inc(s_const, 1)
            pool.wait_ge(s_nat, 16 * NATS)
            pool.tensor_copy(natf[:, 0, :, :], nat[:, 0, :, :]).then_inc(s_natf, 1)
            pool.tensor_copy(natf[:, 1, :, :], nat[:, 1, :, :]).then_inc(s_pool, 1)
            pool.wait_ge(s_pool, 3)
            pool.tensor_scalar(base_f[:, :], natf[:, 1, :, 0], 0.0, None, ALU.max).then_inc(s_pool, 1)
            pool.wait_ge(s_pool, 4)
            pool.tensor_tensor(natf[:, 1, :, :], natf[:, 1, :, :],
                               base_f[:, :].unsqueeze(2).to_broadcast([P, CBLK, CHUNK]),
                               ALU.subtract).then_inc(s_natf, 1)
            pool.wait_ge(s_natf, 2)
            d = natf[:, 1, :, :].rearrange("p b e -> p (b e)")
            over = nat[:, 0, :, :].rearrange("p b e -> p (b e)").bitcast(f32)
            under = nat[:, 1, :, :].rearrange("p b e -> p (b e)").bitcast(f32)
            pool.tensor_scalar(under, d, 0.0, None, ALU.is_lt)
            pool.tensor_scalar(over, d, PAD / 2, None, ALU.is_gt).then_inc(s_pool, 1)
            pool.wait_ge(s_pool, 5)
            pool.tensor_tensor(under, under, over, ALU.mult).then_inc(s_pool, 1)
            pool.wait_ge(s_pool, 6)
            pool.tensor_scalar(over, d, float(WIN - 1), None, ALU.is_gt).then_inc(s_pool, 1)
            pool.wait_ge(s_pool, 7)
            pool.tensor_tensor(under, under, over, ALU.add).then_inc(s_marked, 1)

            pool.wait_ge(s_hd, 16 * HD)

            def gather(k, tiles):
                for j in range(tiles):
                    pool.indirect_dma_start(
                        out=rows[:, k, 0, j, :], out_offset=None, in_=h_dram,
                        in_offset=bass.IndirectOffsetOnAxis(ap=idx[:, k, j:j + 1], axis=0)).then_inc(s_gath[k], 16)

            for k in range(2):
                pool.wait_ge(s_idx[k], 1)
                gather(k, TILES)
            with pool.Fori(2, GROUPS // 2) as v:
                for k in range(2):
                    pool.wait_ge(s_hd, 16 * HD)
                    pool.wait_ge(s_idx[k], v)
                    gather(k, TILES)
            pool.wait_ge(s_idx[0], GROUPS // 2)
            gather(0, TILES)
            pool.wait_ge(s_idx[1], GROUPS // 2)
            gather(1, 2 * TAILC)

            pool.wait_ge(s_flag, 1)
            f = pool.value_load(flag[0:1, 0:1], min_val=0, max_val=P)
            with pool.If(f > 0):
                with pool.Fori(1, E // SLOW + 1) as v:
                    pool.wait_ge(s_hd, 16 * HD)
                    pool.wait_ge(s_fin, v)
                    pool.indirect_dma_start(
                        out=slow_rows[:, 0, :], out_offset=None, in_=h_dram,
                        in_offset=bass.IndirectOffsetOnAxis(ap=slow_idx[:, 0:1], axis=0)).then_inc(s_fg, 16)

            pool.wait_ge(s_hTc, HALF * PAIRS)
            pool.wait_ge(s_wc, WC)
            for q in range(PAIRS):
                t0, t1 = 2 * q * HALF, min((2 * q + 2) * HALF, NT)
                pool.tensor_tensor(xh[:, 0, t0:t1, :], xh[:, 0, t0:t1, :], xh[:, 1, t0:t1, :], ALU.add).then_inc(s_xs1, 1)
                pool.wait_ge(s_xs1, q + 1)
                pool.tensor_tensor(xh[:, 0, t0:t1, :], xh[:, 0, t0:t1, :],
                                   bo_all[:, :].unsqueeze(1).to_broadcast([P, t1 - t0, H]), ALU.add).then_inc(s_xs, 1)

        @block.scalar
        def _(act):
            act.dma_start(wl0[:, :], w1_0).then_inc(s_w, 16)
            act.dma_start(wn0[H:P, :], w2_0[0:H, :]).then_inc(s_w, 16)
            act.dma_start(w2a_s[:, :], w2_0[H:2 * H, :]).then_inc(s_w, 16)
            act.dma_start(w2u_s[:, :], w2_0[2 * H:3 * H, :]).then_inc(s_w, 16)
            act.dma_start(w1o_s[:, :], w1_o).then_inc(s_w, 16)
            act.dma_start(w2o_s[:, :], w2_o).then_inc(s_w, 16)
            act.dma_start(bo_row[:, :], b2_o.rearrange("(o d) -> o d", o=1)).then_inc(s_w, 16)
            with nc.allow_non_contiguous_dma("vectors of 64 onto the partitions"):
                for k, v in enumerate((g1, be1, b1_o, None, g2, be2)):
                    v = u[0, :] if v is None else v
                    act.dma_start(col[:, k:k + 1], v.rearrange("(d o) -> d o", o=1)).then_inc(s_w, 16)
                for lo in (0, H):
                    for k, v in enumerate((b1_0, b1_1, b1_2)):
                        act.dma_start(bias1[lo:lo + H, k:k + 1], v.rearrange("(d o) -> d o", o=1)).then_inc(s_w, 16)
                    for k, v in enumerate((b2_0, b2_1, b2_2)):
                        act.dma_start(bias2[lo:lo + H, k:k + 1], v.rearrange("(d o) -> d o", o=1)).then_inc(s_w, 16)
                act.wait_ge(s_zero, 1)
                act.dma_start(base_row[0:1, 0:REALC],
                              dst.rearrange("(o e) -> o e", o=1)[:, 0:(REALC - 1) * CHUNK + 1:CHUNK]).then_inc(s_w, 16)
            act.wait_ge(s_wz, 7)
            for lo in (0, H):
                for w, a in ((wl0h, w1_0[0:H, :]), (wl0e, w1_0[H:2 * H, :]), (wl1, w1_1), (wl2, w1_2), (wn1, w2_1), (wn2, w2_2)):
                    act.dma_start(w[lo:lo + H, lo:lo + H], a).then_inc(s_w, 16)

            act.wait_ge(s_const, 1)
            for i, (b0, b1) in enumerate(PIECES):
                act.wait_ge(s_lvar, i + 1)
                root_step(P, (b1 - b0) * HALF).then_inc(s_lroot, 1)
            for n in range(TABS):
                k, q = divmod(n, TABK)
                act.wait_ge(s_tabp, n + 1)
                tab = (src_tab, dst_tab)[k]
                b0, b1 = 2 * q, min(2 * q + 2, CBLK)
                act.activation(tab[:, b0 * P:b1 * P, :].rearrange("p (b c) t -> p b t c", c=P),
                               ps_tab[n % 4][:, 0:(b1 - b0) * 2 * P].rearrange("p (b t c) -> p b t c", t=2, c=P),
                               ACT.Copy).then_inc(s_tabc, 1)
            act.wait_ge(s_tabc, TABK)
            for g in range(2):
                act.activation(idx[:, g, :], src_tab[:, g * CPG:(g + 1) * CPG, :].rearrange("p c t -> p (c t)"),
                               ACT.Copy).then_inc(s_idx[g], 1)
            for n in range(PAIRS):
                act.wait_ge(s_hT, n + 1)
                nb = min(2, NBLK - 2 * n)
                cols = node_in[H:P, 2 * n * NODES:(2 * n + nb) * NODES].rearrange("d (g p e) -> d e g p", p=P, e=HALF)
                for t in range(HALF):
                    act.activation(cols[:, t, :, :],
                                   ps_agg[n % 2][t % 2 * H:t % 2 * H + H, 0:nb * 2 * P]
                                   .rearrange("d (b k p) -> d k b p", b=nb, k=2)[:, t // 2, :, :],
                                   ACT.Copy).then_inc(s_hTc, 1)
            act.wait_ge(s_flagp, 1)
            act.activation(flag[0:1, 0:1], ps_l2[0:1, 0:1], ACT.Copy).then_inc(s_flag, 1)

            def edge_iter(i, k, opens, mid, late, stage, after):
                if opens:
                    act.wait_ge(s_tra, i + 1)
                    act.activation(xT[:, 0:GROUP // 2], ps_ta[:, :], ACT.Copy).then_inc(s_xa, 1)
                if stage:
                    act.activation(idx[:, k, :], src_tab[:, bass.ds(i * CPG + 2 * CPG, CPG), :]
                                   .rearrange("p c t -> p (c t)"), ACT.Copy).then_inc(s_idx[k], 1)
                if mid:
                    act.wait_ge(s_l2, i)
                    if late:
                        act.wait_ge(s_t2, i - 1)
                    act.activation(h2[:, :], ps_l2[:, :], ACT.Relu, bias=bias1[:, 2:3]).then_inc(s_h2, 1)
                if late:
                    act.wait_ge(s_rd, i - 1)
                    if late > 1:
                        act.wait_ge(s_agg, i - 3)
                    for q in range(TILES):
                        last = act.activation(cen[:, k, q, 0:H - 1], ps_t2[:, q * H:(q + 1) * H - 1], ACT.Identity,
                                              scale=st[:, 5, q:q + 1], bias=st[:, 0, q:q + 1])
                    last.then_inc(s_cen, 1)
                if opens:
                    act.wait_ge(s_l0, i + 1)
                    if mid:
                        act.wait_ge(s_l1, i)
                    act.activation(h0[:, :], ps_l0[:, :], ACT.Relu, bias=bias1[:, 0:1]).then_inc(s_h0, 1)
                    act.wait_ge(s_l1, i + 1)
                    act.activation(h1[:, :], ps_l1[:, :], ACT.Relu, bias=bias1[:, 1:2]).then_inc(s_h1, 1)
                if after:
                    act.wait_ge(s_trb, i + 2)
                    act.activation(xT[:, GROUP // 2:GROUP], ps_tb[:, :], ACT.Copy).then_inc(s_xb, 1)
                if mid:
                    act.wait_ge(s_var, i)
                    root_step(P, TILES).then_inc(s_root, 1)

            act.wait_ge(s_w, 16 * WS)
            act.wait_ge(s_trb, 1)
            act.activation(xT[:, GROUP // 2:GROUP], ps_tb[:, :], ACT.Copy).then_inc(s_xb, 1)
            edge_iter(0, 0, True, False, 0, True, True)
            edge_iter(1, 1, True, True, 0, True, True)
            edge_iter(2, 0, True, True, 1, True, True)
            edge_iter(3, 1, True, True, 1, True, True)
            with act.Fori(4, GROUPS - 2, 2) as i:
                for k in range(2):
                    edge_iter(i + k, k, True, True, 2, True, True)
            edge_iter(GROUPS - 2, 0, True, True, 2, False, True)
            edge_iter(GROUPS - 1, 1, True, True, 2, False, False)
            edge_iter(GROUPS, 0, False, True, 2, False, False)
            edge_iter(GROUPS + 1, 1, False, False, 2, False, False)

            act.wait_ge(s_flag, 1)
            f = act.value_load(flag[0:1, 0:1], min_val=0, max_val=P)
            with act.If(f > 0):
                with act.Fori(1, E // SLOW + 1) as v:
                    act.wait_ge(s_fg, v * 16)
                    act.sem_inc(s_frow, 1)
                    act.wait_ge(s_fT, v)
                    act.activation(xT[:, 0:SLOW], ps_ta[:, 0:SLOW], ACT.Copy).then_inc(s_fx, 1)
                    for k, (ps, h) in enumerate(((ps_l0, h0), (ps_l1, h1), (ps_l2, h2))):
                        act.wait_ge(s_fl[k], v)
                        act.activation(h[0:H, 0:SLOW], ps[0:H, 0:SLOW], ACT.Relu, bias=bias1[0:H, k:k + 1]).then_inc(s_fh[k], 1)
                    act.wait_ge(s_fvar, v)
                    root_step(SLOW, 1).then_inc(s_froot, 1)

            act.wait_ge(s_wc, WC)
            for q in range(PAIRS + 1):
                if q < PAIRS:
                    act.wait_ge(s_n0, q + 1)
                    if q:
                        act.wait_ge(s_n1, q)
                    act.activation(h0[:, :], ps_l0[:, :], ACT.Relu, bias=bias2[:, 0:1]).then_inc(s_nh0, 1)
                if q:
                    act.wait_ge(s_n2, q)
                    if q > 1:
                        act.wait_ge(s_no, q - 1)
                    act.activation(h2[:, :], ps_l2[:, :], ACT.Relu, bias=bias2[:, 2:3]).then_inc(s_nh2, 1)
                if q < PAIRS:
                    act.wait_ge(s_n1, q + 1)
                    if q:
                        act.wait_ge(s_n2, q)
                    act.activation(h1[:, :], ps_l1[:, :], ACT.Relu, bias=bias2[:, 1:2]).then_inc(s_nh1, 1)
                if q:
                    act.wait_ge(s_nvar, q)
                    root_step(P, TILES).then_inc(s_nroot, 1)

        @block.vector
        def _(dve):
            dve.memset(base_row[:, :], 0).then_inc(s_zero, 1)
            dve.memset(xh[:, :, (NBLK - 1) * HALF:NT, :], 0.0).then_inc(s_zero, 1)
            chain = [0]

            def link(ins):
                chain[0] += 1
                ins.then_inc(s_dve, 1)
                dve.wait_ge(s_dve, chain[0])

            for i, (b0, b1) in enumerate(PIECES):
                t0, tiles = b0 * HALF, (b1 - b0) * HALF
                dve.wait_ge(s_x[i], 16 * XS[i])
                if i == 0:
                    dve.wait_ge(s_zero, 2)
                for t in range(tiles):
                    last = nc.vector.bn_stats(bn[:, t, :], xh[:, 0, t0 + t, :])
                link(last)
                mean_steps(link, P, tiles)
                var_step(P, tiles).then_inc(s_lvar, 1)
                link(nc.vector.tensor_tensor(xh[:, 1, t0:t0 + tiles, :], xh[:, 0, t0:t0 + tiles, :],
                                             st[:, 1, 0:tiles].unsqueeze(2).to_broadcast([P, tiles, H]), ALU.subtract))
                dve.wait_ge(s_lroot, i + 1)
                rstd_steps(link, P, tiles)
                nc.vector.scalar_tensor_tensor(xh[:, 1, t0:t0 + tiles, :], xh[:, 1, t0:t0 + tiles, :], 0.0,
                                               st[:, 5, 0:tiles].unsqueeze(2).to_broadcast([P, tiles, H]),
                                               ALU.max, ALU.mult).then_inc(s_ln, 1)

            dve.wait_ge(s_ln, len(PIECES))
            dve.wait_ge(s_w, 16 * WS)
            dve.wait_ge(s_const, 1)
            link(nc.vector.tensor_scalar(lnw[:, 0, :], drop63[:, :], col[:, 0:1], None, ALU.mult))
            nc.vector.tensor_copy(lnw[:, 0, H - 1:H], col[:, 1:2]).then_inc(s_wc, 1)
            dve.wait_ge(s_wp, 1)
            link(nc.vector.tensor_copy(lnw[:, 1, :], ps_t2[0:H, 0:H]))
            nc.vector.tensor_tensor(lnw[:, 1, H - 1:H], lnw[:, 1, H - 1:H], col[:, 2:3], ALU.add).then_inc(s_wc, 1)
            dve.wait_ge(s_wp, 2)
            nc.vector.tensor_copy(wn0[0:H, :], ps_t2[0:H, 64:64 + H])
            nc.vector.tensor_tensor(bias2[0:H, 0:1], bias2[0:H, 0:1], ps_t2[0:H, 128:129], ALU.add)
            nc.vector.tensor_tensor(bias2[H:P, 0:1], bias2[H:P, 0:1], ps_t2[H:P, 128:129], ALU.add)
            link(nc.vector.tensor_tensor(bo_row[:, :], bo_row[:, :], ps_t2[0:1, 256:256 + H], ALU.add))
            nc.vector.tensor_scalar(w2o_s[:, :], w2o_s[:, :], col[:, 4:5], None, ALU.mult).then_inc(s_wc, 1)
            dve.wait_ge(s_wp, 3)
            nc.vector.tensor_copy(wno[0:H, 0:H], ps_t2[0:H, 320:320 + H])
            nc.vector.tensor_copy(wno[H:P, H:P], ps_t2[H:P, 320:320 + H])
            nc.vector.tensor_copy(bo_all[:, :], ps_t2[:, 384:384 + H]).then_inc(s_wc, 1)

            dve.wait_ge(s_marked, 1)
            nc.vector.tensor_reduce(bad[:, :], nat[:, 1, :, :].rearrange("p b e -> p (b e)").bitcast(f32),
                                    AX.X, ALU.max).then_inc(s_bad, 1)

            dve.memset(cen[:, :, :, H - 1], 1.0)
            dve.memset(node_in[0:H, :], 0.0)
            dve.memset(node_in[H:P, NBLK * NODES:AGGW], 0.0).then_inc(s_zero, 1)
            dve.wait_ge(s_zero, 3)

            base_regs = [dve.alloc_register(f"window_base{c}") for c in range(CPG)]

            def edge_iter(i, k, mid, agg):
                if agg:
                    a = i - 2
                    dve.reg_load(base_regs, base_row[0:1, bass.ds(a * CPG, CPG)])
                    bases = [dve.snap(reg, min_val=0, max_val=N - 1) for reg in base_regs]
                if mid:
                    m = i - 1
                    b = 1 - k
                    step = [0]

                    def link(ins):
                        step[0] += 1
                        ins.then_inc(s_st, 1)
                        dve.wait_ge(s_st, m * 8 + step[0])

                    dve.wait_ge(s_t2, i)
                    ps = ps_t2[:, :].rearrange("p (q d) -> p q d", d=H)
                    for q in range(TILES):
                        last = nc.vector.bn_stats(bn[:, q, :], ps[:, q, :])
                    link(last)
                    if agg:
                        dve.wait_ge(s_cen, i - 1)
                    mean_steps(link, P, TILES)
                    var_step(P, TILES).then_inc(s_var, 1)
                    if agg > 1:
                        dve.wait_ge(s_agg, i - 2)
                    nc.vector.tensor_tensor(
                        onehot[:, b, :, :], iota[:, :].unsqueeze(1).to_broadcast([P, TILES, WIN]),
                        dst_tab[:, bass.ds(m * CPG, CPG), :].rearrange("p c t -> p (c t)").unsqueeze(2)
                        .to_broadcast([P, TILES, WIN]), ALU.is_equal).then_inc(s_oh, 1)
                if agg:
                    dve.wait_ge(s_agg, i - 1)
                    for c in range(CPG):
                        if agg > 1 or c:
                            dve.wait_ge(s_add, a * CPG + c)
                        win = node_in[0:H, bass.ds(bases[c], WIN)]
                        nc.vector.tensor_tensor(win, win, ps_agg[k][0:H, c * WIN:(c + 1) * WIN], ALU.add).then_inc(s_add, 1)
                if mid:
                    dve.wait_ge(s_root, i)
                    rstd_steps(link, P, TILES)
                    nc.vector.scalar_tensor_tensor(st[:, 0, 0:TILES], st[:, 1, 0:TILES], -1.0, st[:, 5, 0:TILES],
                                                   ALU.mult, ALU.mult).then_inc(s_rd, 1)

            edge_iter(1, 1, True, 0)
            edge_iter(2, 0, True, 1)
            edge_iter(3, 1, True, 2)
            with dve.Fori(4, GROUPS, 2) as i:
                for k in range(2):
                    edge_iter(i + k, k, True, 2)
            edge_iter(GROUPS, 0, True, 2)
            edge_iter(GROUPS + 1, 1, False, 2)

            dve.wait_ge(s_flag, 1)
            dve.wait_ge(s_add, CHUNKS)
            f = dve.value_load(flag[0:1, 0:1], min_val=0, max_val=P)
            with dve.If(f > 0):
                dve.memset(node_in[0:H, :], 0.0).then_inc(s_fz, 1)
                dve.wait_ge(s_fz, 1)
                dve.sem_inc(s_fd, 1)
                dve.sem_inc(s_fadd, 1)
                with dve.Fori(1, E // SLOW + 1) as v:
                    step = [0]

                    def link(ins):
                        step[0] += 1
                        ins.then_inc(s_fs, 1)
                        dve.wait_ge(s_fs, v * 8 - 8 + step[0])

                    dve.wait_ge(s_fU, v)
                    link(nc.vector.bn_stats(bn[0:SLOW, 0, :], ps_t2[0:SLOW, 0:H]))
                    mean_steps(link, SLOW, 1)
                    nc.vector.tensor_scalar(slow_cen[:, :], ps_t2[0:SLOW, 0:H], st[0:SLOW, 1, 0:1], None, ALU.subtract)
                    var_step(SLOW, 1).then_inc(s_fvar, 1)
                    dve.wait_ge(s_froot, v)
                    rstd_steps(link, SLOW, 1)
                    nc.vector.scalar_tensor_tensor(slow_cen[:, H - 1:H], st[0:SLOW, 4, 0:1], EPS,
                                                   st[0:SLOW, 5, 0:1], ALU.add, ALU.mult)
                    nc.vector.tensor_scalar(slow_diag[:, :], ident[0:SLOW, 0:SLOW], st[0:SLOW, 5, 0:1],
                                            None, ALU.mult).then_inc(s_frd, 1)
                    dve.wait_ge(s_fm, v)
                    nc.vector.tensor_copy(slow_msg[:, :], ps_tb[0:H, 0:SLOW]).then_inc(s_fc, 1)
                    dve.wait_ge(s_fz, 1)
                    dve.wait_ge(s_fc, v)
                    with dve.Fori(0, SLOW) as e:
                        node = dve.value_load(slow_dst[0:1, bass.ds(e, 1)], min_val=0, max_val=N - 1)
                        dve.wait_ge(s_fadd, v * SLOW + e - (SLOW - 1))
                        c = node_in[0:H, bass.ds(node, 1)]
                        nc.vector.tensor_tensor(c, c, slow_msg[:, bass.ds(e, 1)], ALU.add).then_inc(s_fadd, 1)
                    dve.wait_ge(s_fadd, v * SLOW + 1)
                    dve.sem_inc(s_fd, 1)
            dve.sem_inc(s_sums, 1)

            for q in range(PAIRS):
                step = [0]

                def link(ins):
                    step[0] += 1
                    ins.then_inc(s_nst, 1)
                    dve.wait_ge(s_nst, q * 8 + step[0])

                dve.wait_ge(s_nt, q + 1)
                ps = ps_t2[:, :].rearrange("p (k h d) -> p (k h) d", h=2, d=H)
                for t in range(TILES):
                    last = nc.vector.bn_stats(bn[:, t, :], ps[:, t, :])
                link(last)
                mean_steps(link, P, TILES)
                var_step(P, TILES).then_inc(s_nvar, 1)
                if q:
                    dve.wait_ge(s_nres, q)
                dve.wait_ge(s_nroot, q + 1)
                rstd_steps(link, P, TILES)
                dve.wait_ge(s_no, q + 1)
                dve.wait_ge(s_xs, q + 1)
                if q >= 2:
                    dve.wait_ge(s_out[q % 2], 16 * (q // 2))
                po = ps_agg[q % 2][:, :].rearrange("p (k h d) -> p k h d", h=2, d=H)
                halves = min(2, NBLK - 2 * q)
                for t in range(HALF):
                    for h in range(halves):
                        j = t * 2 + h
                        last = nc.vector.scalar_tensor_tensor(
                            res[:, q % 2, h * HALF + t, :], po[:, t, h, :], st[:, 5, j:j + 1],
                            xh[:, 0, (2 * q + h) * HALF + t, :], ALU.mult, ALU.add)
                last.then_inc(s_nres, 1)

        @block.tensor
        def _(pe):
            pe.wait_ge(s_const, 1)
            for n in range(TABS):
                k, q = divmod(n, TABK)
                if q == 0:
                    pe.wait_ge(s_natf, k + 1)
                if n >= 4:
                    pe.wait_ge(s_tabc, n - 3)
                for b in range(2 * q, min(2 * q + 2, CBLK)):
                    for t in range(2):
                        o = (b - 2 * q) * 2 * P + t * P
                        last = pe.transpose(ps_tab[n % 4][:, o:o + P],
                                            natf[:, k, b, :].rearrange("c (p t) -> c t p", t=2)[:, t, :], ident[:, :])
                last.then_inc(s_tabp, 1)
            for n in range(PAIRS):
                nb = min(2, NBLK - 2 * n)
                pe.wait_ge(s_ln, (2 * n + nb - 1) // PIECE + 1)
                if n >= 2:
                    pe.wait_ge(s_hTc, HALF * (n - 1))
                for k in range(2 * nb):
                    t = 2 * n * HALF + 2 * k
                    last = pe.transpose(ps_agg[n % 2][:, k * P:(k + 1) * P],
                                        xh[:, 1, t:t + 2, :].rearrange("p t d -> p (t d)"), ident[:, :])
                last.then_inc(s_hT, 1)
            pe.wait_ge(s_w, 16 * WS)
            pe.wait_ge(s_wc, 1)
            pe.matmul(ps_t2[0:H, 0:H], w1o_s[:, :], lnw[:, 0, :], start=True, stop=True).then_inc(s_wp, 1)
            pe.wait_ge(s_wc, 2)
            pe.matmul(ps_t2[0:H, 64:64 + H], lnw[:, 1, :], w2a_s[:, :], start=True, stop=True)
            pe.matmul(ps_t2[0:H, 128:129], w2u_s[:, :], col[:, 3:4], start=True, stop=True)
            pe.matmul(ps_t2[H:P, 128:129], w2u_s[:, :], col[:, 3:4], start=True, stop=True)
            pe.matmul(ps_t2[0:1, 256:256 + H], col[:, 5:6], w2o_s[:, :], start=True, stop=True).then_inc(s_wp, 1)
            pe.wait_ge(s_wc, 3)
            pe.matmul(ps_t2[0:H, 320:320 + H], lnw[:, 2, :], w2o_s[:, :], start=True, stop=True)
            pe.matmul(ps_t2[H:P, 320:320 + H], lnw[:, 2, :], w2o_s[:, :], start=True, stop=True)
            pe.matmul(ps_t2[:, 384:384 + H], one_row[:, :], bo_row[:, :], start=True, stop=True).then_inc(s_wp, 1)
            pe.wait_ge(s_bad, 1)
            pe.matmul(ps_l2[0:1, 0:1], bad[:, :], ones[:, :], start=True, stop=True).then_inc(s_flagp, 1)
            pe.wait_ge(s_wc, WC)
            pe.wait_ge(s_hTc, HALF * PAIRS)
            pe.wait_ge(s_flag, 1)
            pe.wait_ge(s_tabc, TABS)
            pe.wait_ge(s_zero, 3)

            def attrs_turned(i, k, attrs, later):
                pe.wait_ge(s_attr[k], attrs)
                if later:
                    pe.wait_ge(s_xb, i)
                for c in range(CPG):
                    last = pe.transpose(ps_tb[:, c * P:(c + 1) * P],
                                        rows[:, k, 1, 2 * c:2 * c + 2, :].rearrange("p t d -> p (t d)"), ident[:, :])
                last.then_inc(s_trb, 1)

            def edge_iter(i, k, opens, mid, agg, gathered, attrs):
                if opens:
                    pe.wait_ge(s_gath[k], gathered)
                    if mid:
                        pe.wait_ge(s_xa, i)
                    for c in range(CPG):
                        last = pe.transpose(ps_ta[:, c * P:(c + 1) * P],
                                            rows[:, k, 0, 2 * c:2 * c + 2, :].rearrange("p t d -> p (t d)"), ident[:, :])
                    last.then_inc(s_tra, 1)
                if mid:
                    pe.wait_ge(s_h1, i)
                    if agg:
                        pe.wait_ge(s_h2, i - 1)
                    pe.matmul(ps_l2[:, :], wl2[:, :], h1[:, :], start=True, stop=True).then_inc(s_l2, 1)
                if opens:
                    if mid:
                        pe.wait_ge(s_h0, i)
                    pe.wait_ge(s_xb, i + 1)
                    pe.matmul(ps_l0[:, :], wl0e[:, :], xT[:, GROUP // 2:GROUP], start=True, stop=False)
                    pe.wait_ge(s_xa, i + 1)
                    pe.matmul(ps_l0[:, :], wl0h[:, :], xT[:, 0:GROUP // 2], start=False, stop=True).then_inc(s_l0, 1)
                if mid:
                    pe.wait_ge(s_h2, i)
                    if agg:
                        pe.wait_ge(s_cen, i - 1)
                    for t in range(HALF):
                        last = pe.transpose(ps_t2[:, t * P:(t + 1) * P], h2[:, t * P:(t + 1) * P], ident[:, :])
                    last.then_inc(s_t2, 1)
                if agg:
                    pe.wait_ge(s_cen, i - 1)
                    pe.wait_ge(s_oh, i - 1)
                    if agg > 1:
                        pe.wait_ge(s_add, (i - 3) * CPG)
                    for c in range(CPG):
                        for t in range(2):
                            last = pe.matmul(ps_agg[k][0:H, c * WIN:(c + 1) * WIN], cen[:, k, 2 * c + t, :],
                                             onehot[:, k, 2 * c + t, :], start=(t == 0), stop=(t == 1))
                    last.then_inc(s_agg, 1)
                if opens:
                    pe.wait_ge(s_h0, i + 1)
                    if mid:
                        pe.wait_ge(s_h1, i)
                    pe.matmul(ps_l1[:, :], wl1[:, :], h0[:, :], start=True, stop=True).then_inc(s_l1, 1)
                if attrs is not None:
                    attrs_turned(i + 1, 1 - k, attrs, True)

            GV = 16 * TILES
            attrs_turned(0, 0, 16, False)
            edge_iter(0, 0, 1, 0, 0, GV, 16)
            edge_iter(1, 1, 1, 1, 0, GV, 32)
            edge_iter(2, 0, 1, 1, 1, 2 * GV, 32)
            edge_iter(3, 1, 1, 1, 1, 2 * GV, 48)
            with pe.Fori(2, GROUPS // 2 - 1) as n:
                edge_iter(n * 2, 0, 1, 1, 2, n * GV + GV, n * 16 + 16)
                edge_iter(n * 2 + 1, 1, 1, 1, 2, n * GV + GV, n * 16 + 32)
            n = GROUPS // 2 - 1
            edge_iter(GROUPS - 2, 0, 1, 1, 2, (n + 1) * GV, n * 16 + 16 * TAILC)
            edge_iter(GROUPS - 1, 1, 1, 1, 2, n * GV + 32 * TAILC, None)
            edge_iter(GROUPS, 0, 0, 1, 2, 0, None)
            edge_iter(GROUPS + 1, 1, 0, 0, 2, 0, None)

            f = pe.value_load(flag[0:1, 0:1], min_val=0, max_val=P)
            with pe.If(f > 0):
                with pe.Fori(1, E // SLOW + 1) as v:
                    pe.wait_ge(s_fz, 1)
                    pe.wait_ge(s_frow, v)
                    pe.transpose(ps_ta[:, 0:SLOW], slow_rows[:, :, :].rearrange("p k d -> p (k d)"),
                                 ident[0:SLOW, 0:SLOW]).then_inc(s_fT, 1)
                    pe.wait_ge(s_fz, 1)
                    pe.wait_ge(s_fx, v)
                    pe.matmul(ps_l0[0:H, 0:SLOW], wl0[:, :], xT[:, 0:SLOW], start=True, stop=True).then_inc(s_fl[0], 1)
                    for k, (ps, w, h) in enumerate(((ps_l1, wl1, h0), (ps_l2, wl2, h1))):
                        pe.wait_ge(s_fz, 1)
                        pe.wait_ge(s_fh[k], v)
                        pe.matmul(ps[0:H, 0:SLOW], w[0:H, 0:H], h[0:H, 0:SLOW], start=True, stop=True).then_inc(s_fl[k + 1], 1)
                    pe.wait_ge(s_fz, 1)
                    pe.wait_ge(s_fh[2], v)
                    pe.transpose(ps_t2[0:SLOW, 0:H], h2[0:H, 0:SLOW], ident[0:H, 0:H]).then_inc(s_fU, 1)
                    pe.wait_ge(s_fz, 1)
                    pe.wait_ge(s_frd, v)
                    pe.matmul(ps_tb[0:H, 0:SLOW], slow_cen[:, :], slow_diag[:, :], start=True, stop=True).then_inc(s_fm, 1)

            pe.wait_ge(s_sums, 1)
            hv = h2[:, :].rearrange("d (p t) -> d t p", t=HALF)
            for q in range(PAIRS + 1):
                if q < PAIRS:
                    c0 = 2 * q * NODES
                    if q:
                        pe.wait_ge(s_nh0, q)
                    for h in range(2):
                        last = pe.matmul(ps_l0[h * H:(h + 1) * H, :], wn0[:, :],
                                         node_in[:, c0 + h * NODES:c0 + (h + 1) * NODES], start=True, stop=True)
                    last.then_inc(s_n0, 1)
                if q:
                    pe.wait_ge(s_nh1, q)
                    if q > 1:
                        pe.wait_ge(s_nh2, q - 1)
                    pe.matmul(ps_l2[:, :], wn2[:, :], h1[:, :], start=True, stop=True).then_inc(s_n2, 1)
                if q < PAIRS:
                    pe.wait_ge(s_nh0, q + 1)
                    if q:
                        pe.wait_ge(s_nh1, q)
                    pe.matmul(ps_l1[:, :], wn1[:, :], h0[:, :], start=True, stop=True).then_inc(s_n1, 1)
                if q:
                    pe.wait_ge(s_nh2, q)
                    if q > 1:
                        pe.wait_ge(s_nvar, q - 1)
                    for t in range(HALF):
                        last = pe.transpose(ps_t2[:, t * P:(t + 1) * P], hv[:, t, :], ident[:, :])
                    last.then_inc(s_nt, 1)
                    if q > 2:
                        pe.wait_ge(s_nres, q - 2)
                    for t in range(HALF):
                        last = pe.matmul(ps_agg[(q - 1) % 2][:, t * P:(t + 1) * P], hv[:, t, :], wno[:, :],
                                         start=True, stop=True)
                    last.then_inc(s_no, 1)


_INS = ['x', 'src', 'dst', 'edge_attr_64', 'L0_gnn_u'] + [
    'L0_gnn_' + n for n in ('w1_0', 'b1_0', 'w1_1', 'b1_1', 'w1_2', 'b1_2', 'g1', 'be1', 'w1_o', 'b1_o',
                            'w2_0', 'b2_0', 'w2_1', 'b2_1', 'w2_2', 'b2_2', 'g2', 'be2', 'w2_o', 'b2_o')]


def kernel(**inputs):
    import numpy as _np
    import concourse.bacc as _bacc
    from concourse import mybir as _mybir
    from concourse.bass_utils import run_bass_kernel_spmd as _run

    nc = _bacc.Bacc("TRN2", target_bir_lowering=False, num_devices=1)
    arrays, args = {}, []
    for name in _INS:
        a = _np.ascontiguousarray(inputs[name])
        arrays[f"in_{name}_dram"] = a
        args.append(nc.dram_tensor(f"in_{name}_dram", a.shape, _mybir.dt.from_np(a.dtype), kind="ExternalInput").ap())
    shape = tuple(inputs['x'].shape)
    h_dram = nc.dram_tensor("h_dram", shape, _mybir.dt.float32).ap()
    out = nc.dram_tensor("out_0_dram", shape, _mybir.dt.float32, kind="ExternalOutput").ap()
    gnn_layer(nc, *args, h_dram, out)
    r = _run(nc, [arrays], core_ids=[0])
    return r.results[0]["out_0_dram"]
```

```python
import concourse.bass as bass
from concourse import mybir
from contextlib import ExitStack


def weight_columns():
    at, c = {}, 0
    for name, n in (("l0h", 128), ("l0e", 128), ("l1", 128), ("l2", 128), ("bias1", 3), ("n1", 128), ("n2", 128),
                    ("l0", 64), ("n0", 64), ("w1o", 64), ("w2a", 64), ("w2u", 64), ("w2o", 64), ("bias2", 3),
                    ("col", 6), ("bo", 64)):
        at[name] = (c, n)
        c += n
    return at, c


def gnn_layer(nc, x, src, dst, edge_attr, packed, out):
    f32, i32 = mybir.dt.float32, mybir.dt.int32
    ALU, ACT, AX = mybir.AluOpType, mybir.ActivationFunctionType, mybir.AxisListType

    P = 128
    N, H = x.shape
    E = src.shape[0]
    EPS = 1e-5
    TILES = 8
    HALF = TILES // 2
    GROUP = TILES * P
    CHUNK = 2 * P
    CPG = GROUP // CHUNK
    WIN = 64
    GROUPS = 2 * -(-E // (2 * GROUP))
    FULL = E // GROUP
    assert FULL == GROUPS - 1 and E % 2 == 0 and GROUPS >= 6
    CHUNKS = GROUPS * CPG
    CBLK = -(-CHUNKS // P)
    NODES = HALF * P
    NBLK = -(-N // NODES)
    LASTP = (N - (NBLK - 1) * NODES) // HALF
    assert (N - (NBLK - 1) * NODES) % HALF == 0 and NBLK > 1
    PAIRS = -(-NBLK // 2)
    NBE = 2 * PAIRS
    AGGW = NBE * NODES + WIN
    T0 = 4
    assert GROUPS > NBE + 9
    PAD = -float(1 << 22)
    SLOW = 64
    assert E % SLOW == 0

    REALC = -(-E // CHUNK)
    TAILC = REALC - FULL * CPG
    TABK = -(-CBLK // 2)
    TABS = 2 * TABK
    NATS = sum(1 for n in (E // (P * CHUNK), E % (P * CHUNK) // CHUNK, E % CHUNK) if n)
    WC = 4
    AT, COLS = weight_columns()
    ALLT = HALF + 2 * TILES
    NODE_T, RAW_T, OUT_T = 0, HALF, HALF + TILES
    ZSPLIT = AGGW * 2 // 5 // 64 * 64
    OUTS = [sum(16 * ((min(2 * q + 2, NBLK) - 2 * q > (2 * q + 2 >= NBLK)) + (2 * q + 2 >= NBLK))
                for q in range(PAIRS) if q % 2 == k) for k in range(2)]

    ctx = ExitStack()
    with ctx:
        def sb(name, shape, dt=f32):
            return ctx.enter_context(nc.sbuf_tensor(name, shape, dt))

        def sem(name):
            return ctx.enter_context(nc.semaphore(name))

        node_in = sb("node_in", [P, AGGW])
        xn = sb("xn", [P, NBE * HALF, H])
        hs = sb("hs", [P, 2, HALF, H])
        nat = sb("nat", [P, 2, CBLK, CHUNK], i32)
        natf = sb("natf", [P, 2, CBLK, CHUNK])
        base_f = sb("base_f", [P, CBLK])
        src_tab = sb("src_tab", [P, CBLK * P, 2], i32)
        dst_tab = sb("dst_tab", [P, CBLK * P, 2])
        base_row = sb("base_row", [1, CHUNKS], i32)
        rows = sb("rows", [P, 2, 2, TILES, H])
        raw = sb("raw", [P, 2, TILES, H])
        idx = sb("idx", [P, 2, TILES], i32)
        xT = sb("xT", [P, GROUP])
        h0 = sb("h0", [P, NODES])
        h1 = sb("h1", [P, NODES])
        h2 = sb("h2", [P, NODES])
        cen = sb("cen", [P, 2, TILES, H])
        onehot = sb("onehot", [P, 2, TILES, WIN])
        bn = sb("bn", [P, ALLT, 6])
        st = sb("st", [P, 7, ALLT])
        rstd = sb("rstd", [P, 2, ALLT])
        shift = sb("shift", [P, 2, TILES])
        zeros = sb("zeros", [H, NODES])
        eps = sb("eps", [P, 1])
        ident = sb("ident", [P, P])
        iota = sb("iota", [P, WIN])
        ones = sb("ones", [P, 1])
        one_row = sb("one_row", [1, P])
        bad = sb("bad", [P, 3])
        flag = sb("flag", [1, 1], i32)
        w = sb("w", [P, COLS])

        def part(name, rows=P):
            c, n = AT[name]
            return w[0:rows, c:c + n]

        wl0h, wl0e, wl1, wl2, wn1, wn2, wl0, wn0, bias1, bias2 = (
            part(n) for n in ("l0h", "l0e", "l1", "l2", "n1", "n2", "l0", "n0", "bias1", "bias2"))
        w1o_s, w2a_s, w2u_s, w2o_s, col = (part(n, H) for n in ("w1o", "w2a", "w2u", "w2o", "col"))
        bo_row = part("bo", 1)
        wno = sb("wno", [P, P])
        drop63 = sb("drop63", [H, H])
        lnw = sb("lnw", [H, 3, H])
        bo_all = sb("bo_all", [P, H])
        res = sb("res", [P, 2, 2 * HALF, H])
        slow_raw = sb("slow_raw", [SLOW, H])
        slow_rows = sb("slow_rows", [SLOW, 2, H])
        slow_idx = sb("slow_idx", [SLOW, 1], i32)
        slow_dst = sb("slow_dst", [1, SLOW], i32)
        slow_cen = sb("slow_cen", [SLOW, H])
        slow_diag = sb("slow_diag", [SLOW, SLOW])
        slow_msg = sb("slow_msg", [H, SLOW])

        def bank(name):
            return ctx.enter_context(nc.psum_tensor(name, [P, 512], f32))

        ps_ta, ps_tb, ps_l0, ps_l1, ps_l2, ps_agg = (bank(n) for n in ("ta", "tb", "l0", "l1", "l2", "agg"))
        ps_t2 = [bank("t2a"), bank("t2b")]
        AW = CPG * WIN
        ps_tab = [ps_ta, ps_tb, ps_l0, ps_l1, ps_l2, ps_t2[0], ps_t2[1]]

        s_ix = sem("s_ix")
        s_nats, s_natd = sem("s_nats"), sem("s_natd")
        s_natm = sem("s_natm")
        s_w, s_base = sem("s_w"), sem("s_base")
        s_x = sem("s_x")
        s_const = sem("s_const")
        s_pool = sem("s_pool")
        s_natf = sem("s_natf")
        s_ln = sem("s_ln")
        s_bad = sem("s_bad")
        s_var, s_root = sem("s_var"), sem("s_root")
        s_nvar, s_nroot = sem("s_nvar"), sem("s_nroot")
        s_fvar, s_froot = sem("s_fvar"), sem("s_froot")
        s_tabp = sem("s_tabp")
        s_tabc = sem("s_tabc")
        s_hT = sem("s_hT")
        s_hTc = sem("s_hTc")
        s_wp = sem("s_wp")
        s_wc = sem("s_wc")
        s_flagp = sem("s_flagp")
        s_flag = sem("s_flag")
        s_free = [sem("s_free0"), sem("s_free1")]
        s_gath = [sem("s_gath0"), sem("s_gath1")]
        s_norm = sem("s_norm")
        s_attr = [sem("s_attr0"), sem("s_attr1")]
        s_tra, s_trb = sem("s_tra"), sem("s_trb")
        s_xa, s_xb = sem("s_xa"), sem("s_xb")
        s_l0, s_l1, s_l2 = sem("s_l0"), sem("s_l1"), sem("s_l2")
        s_h0, s_h1, s_h2 = sem("s_h0"), sem("s_h1"), sem("s_h2")
        s_t2 = sem("s_t2")
        s_rd = sem("s_rd")
        s_cen = sem("s_cen")
        s_oh = sem("s_oh")
        s_agg = sem("s_agg")
        s_add = sem("s_add")
        s_dve = sem("s_dve")
        s_st = sem("s_st")
        s_zero, s_zeroa = sem("s_zero"), sem("s_zeroa")
        s_fz, s_fload, s_fin, s_fg, s_frow, s_fT, s_fx, s_fU, s_fs, s_frd, s_fm, s_fc, s_fadd, s_fd = (
            sem("s_f_" + n) for n in ("zero", "load", "in", "gath", "row", "T", "x", "U", "chain", "rd", "m",
                                      "c", "add", "done"))
        s_fl, s_fh = [sem(f"s_fl{k}") for k in range(3)], [sem(f"s_fh{k}") for k in range(3)]
        s_sums = sem("s_sums")
        s_n0, s_n1, s_n2, s_nt, s_no = (sem(f"s_n{k}") for k in "012to")
        s_nh0, s_nh1, s_nh2 = (sem(f"s_nh{k}") for k in "012")
        s_nst, s_nres = sem("s_nst"), sem("s_nres")
        s_xs = sem("s_xs")
        s_out = [sem("s_out0"), sem("s_out1")]

        def attr_rows(e0, chunks, parts):
            return edge_attr[bass.ds(e0, (chunks - 1) * CHUNK + 2 * parts), :].rearrange(
                "(c p t) d -> p c (t d)", c=chunks, t=2)

        def node_rows(t, b0, b1):
            return t[b0 * NODES:b1 * NODES, :].rearrange("(b p t) d -> p b (t d)", p=P, t=HALF)

        def node_tail(t):
            return t[(NBLK - 1) * NODES:N, :].rearrange("(p t) d -> p (t d)", t=HALF)

        block = ctx.enter_context(nc.Block())

        def span(i):
            if not isinstance(i, int) or i >= T0:
                return NODE_T, ALLT
            return RAW_T, ALLT if i > 0 else OUT_T

        def mean_steps(link, parts, lo, hi):
            b = bn[0:parts, lo:hi, :]
            s = st[0:parts, :, lo:hi]
            link(nc.vector.tensor_tensor(s[:, 0, :], b[:, :, 1], b[:, :, 4], ALU.subtract))
            nc.vector.scalar_tensor_tensor(s[:, 2, :], s[:, 0, :], 0.25, s[:, 0, :], ALU.mult, ALU.mult)
            nc.vector.tensor_tensor(s[:, 3, :], b[:, :, 2], b[:, :, 5], ALU.add)
            link(nc.vector.scalar_tensor_tensor(s[:, 1, :], s[:, 0, :], -0.5, b[:, :, 1], ALU.mult, ALU.add))

        def var_step(parts, lo, hi):
            s = st[0:parts, :, lo:hi]
            return nc.vector.scalar_tensor_tensor(s[:, 4, :], s[:, 3, :], 1.0 / H, s[:, 2, :], ALU.mult, ALU.add)

        def root_step(parts, lo, hi):
            return nc.scalar.activation(st[0:parts, 5, lo:hi], st[0:parts, 4, lo:hi], ACT.Sqrt, bias=eps[0:parts, :])

        def rstd_steps(link, parts, lo, hi, k):
            s = st[0:parts, :, lo:hi]
            link(nc.vector.reciprocal(s[:, 5, :], s[:, 5, :]))
            link(nc.vector.tensor_tensor(s[:, 6, :], s[:, 5, :], s[:, 5, :], ALU.mult))
            link(nc.vector.scalar_tensor_tensor(s[:, 6, :], s[:, 4, :], EPS, s[:, 6, :], ALU.add, ALU.mult))
            link(nc.vector.tensor_scalar(s[:, 6, :], s[:, 6, :], -0.5, 1.5, ALU.mult, ALU.add))
            link(nc.vector.tensor_tensor(rstd[0:parts, k, lo:hi], s[:, 5, :], s[:, 6, :], ALU.mult))

        @block.sync
        def _(sp):
            for g in range(2):
                sp.dma_start(idx[:, g, :].rearrange("p (c t) -> p c t", t=2),
                             src[g * GROUP:(g + 1) * GROUP].rearrange("(c p t) -> p c t", p=P, t=2)).then_inc(s_ix, 16)
            sp.wait_ge(s_natm, 2)
            full = E // (P * CHUNK)
            rest = (E - full * P * CHUNK) // CHUNK
            left = E - (full * P + rest) * CHUNK
            for k, (a, landed) in enumerate(((src, s_nats), (dst, s_natd))):
                if full:
                    sp.dma_start(nat[:, k, 0:full, :],
                                 a[0:full * P * CHUNK].rearrange("(b p e) -> p b e", p=P, e=CHUNK)).then_inc(landed, 16)
                if rest:
                    sp.dma_start(nat[0:rest, k, full, :],
                                 a[full * P * CHUNK:(full * P + rest) * CHUNK].rearrange("(p e) -> p e", e=CHUNK)
                                 ).then_inc(landed, 16)
                if left:
                    sp.dma_start(nat[rest:rest + 1, k, full, 0:left],
                                 a[E - left:E].rearrange("(p e) -> p e", p=1)).then_inc(landed, 16)
            for g in range(2):
                sp.dma_start(rows[:, g, 1, :, :].rearrange("p (c t) d -> p c (t d)", t=2),
                             attr_rows(g * GROUP, CPG, P)).then_inc(s_attr[g], 16)
            sp.wait_ge(s_zero, 1)
            with nc.allow_non_contiguous_dma("one value of each chunk"):
                sp.dma_start(base_row[0:1, 0:REALC],
                             dst.rearrange("(o e) -> o e", o=1)[:, 0:(REALC - 1) * CHUNK + 1:CHUNK]).then_inc(s_base, 16)
            sp.wait_ge(s_zero, 2)
            sp.dma_start(xn[:, 0:(NBLK - 1) * HALF, :].rearrange("p (b t) d -> p b (t d)", t=HALF),
                         node_rows(x, 0, NBLK - 1)).then_inc(s_x, 16)
            sp.dma_start(xn[0:LASTP, (NBLK - 1) * HALF:NBLK * HALF, :].rearrange("p t d -> p (t d)"),
                         node_tail(x)).then_inc(s_x, 16)

            with sp.Fori(2, GROUPS - 2, 2) as g:
                for k in range(2):
                    sp.wait_ge(s_trb, g + k - 1)
                    sp.dma_start(rows[:, k, 1, :, :].rearrange("p (c t) d -> p c (t d)", t=2),
                                 attr_rows(g * GROUP + k * GROUP, CPG, P)).then_inc(s_attr[k], 16)
            g = GROUPS - 2
            sp.wait_ge(s_trb, g - 1)
            sp.dma_start(rows[:, 0, 1, :, :].rearrange("p (c t) d -> p c (t d)", t=2),
                         attr_rows(g * GROUP, CPG, P)).then_inc(s_attr[0], 16)
            g = GROUPS - 1
            sp.wait_ge(s_trb, g - 1)
            for c in range(TAILC):
                n = min(CHUNK, E - g * GROUP - c * CHUNK) // 2
                sp.dma_start(rows[0:n, 1, 1, 2 * c:2 * c + 2, :].rearrange("p t d -> p (t d)"),
                             attr_rows(g * GROUP + c * CHUNK, 1, n).rearrange("p c d -> p (c d)")).then_inc(s_attr[1], 16)

            sp.wait_ge(s_flag, 1)
            f = sp.value_load(flag[0:1, 0:1], min_val=0, max_val=P)
            with sp.If(f > 0):
                with sp.Fori(1, E // SLOW + 1) as v:
                    sp.wait_ge(s_fd, v)
                    e0 = v * SLOW - SLOW
                    sp.dma_start(slow_idx[:, :], src[bass.ds(e0, SLOW)].rearrange("(p o) -> p o", o=1)).then_inc(s_fload, 16)
                    sp.dma_start(slow_dst[:, :], dst[bass.ds(e0, SLOW)].rearrange("(o e) -> o e", o=1)).then_inc(s_fload, 16)
                    sp.dma_start(slow_rows[:, 1, :], edge_attr[bass.ds(e0, SLOW), :]).then_inc(s_fload, 16)
                    sp.wait_ge(s_fload, v * 48)
                    sp.sem_inc(s_fin, 1)

            for q in range(PAIRS):
                sp.wait_ge(s_nres, q + 1)
                b0, b1 = 2 * q, min(2 * q + 2, NBLK)
                fb = b1 - 1 if b1 == NBLK else b1
                if fb > b0:
                    sp.dma_start(node_rows(out, b0, fb),
                                 res[:, q % 2, 0:(fb - b0) * HALF, :].rearrange("p (b t) d -> p b (t d)", t=HALF)
                                 ).then_inc(s_out[q % 2], 16)
                if b1 == NBLK:
                    sp.dma_start(node_tail(out), res[0:LASTP, q % 2, (fb - b0) * HALF:(fb - b0 + 1) * HALF, :]
                                 .rearrange("p t d -> p (t d)")).then_inc(s_out[q % 2], 16)
            for k in range(2):
                sp.wait_ge(s_out[k], OUTS[k])

        @block.gpsimd
        def _(pool):
            pool.memset(nat[:, 0, CBLK - 1, :], 0).then_inc(s_natm, 1)
            pool.memset(nat[:, 1, CBLK - 1, :], int(PAD)).then_inc(s_natm, 1)
            pool.memset(ident[:, :], 0.0)
            pool.memset(drop63[:, :], 0.0)
            pool.memset(ones[:, :], 1.0)
            pool.memset(eps[:, :], EPS)
            pool.memset(one_row[:, :], 1.0)
            pool.memset(lnw[:, 2, :], -1.0 / H)
            pool.iota(iota[:, :], pattern=[[1, WIN]], base=0, channel_multiplier=0,
                      allow_small_or_imprecise_dtypes=True).then_inc(s_pool, 1)
            pool.wait_ge(s_pool, 1)
            pool.affine_select(out=ident[:, :], in_=ident[:, :], compare_op=ALU.not_equal, fill=1.0,
                               base=0, pattern=[[-1, P]], channel_multiplier=1)
            pool.affine_select(out=drop63[:, :], in_=drop63[:, :], compare_op=ALU.not_equal, fill=-1.0,
                               base=1 - H, pattern=[[0, H]], channel_multiplier=1).then_inc(s_pool, 1)
            pool.wait_ge(s_pool, 2)
            pool.affine_select(out=drop63[:, :], in_=drop63[:, :], compare_op=ALU.not_equal, fill=1.0,
                               base=0, pattern=[[-1, H]], channel_multiplier=1)
            pool.tensor_tensor(lnw[:, 2, :], lnw[:, 2, :], ident[0:H, 0:H], ALU.add).then_inc(s_const, 1)

            def gather(k, tiles):
                for j in range(tiles):
                    pool.indirect_dma_start(
                        out=raw[:, k, j, :], out_offset=None, in_=x,
                        in_offset=bass.IndirectOffsetOnAxis(ap=idx[:, k, j:j + 1], axis=0)).then_inc(s_gath[k], 16)

            pool.wait_ge(s_ix, 32)
            gather(0, TILES)
            gather(1, TILES)
            with pool.Fori(1, GROUPS // 2 - 1) as v:
                for k in range(2):
                    pool.wait_ge(s_ix, 32)
                    pool.wait_ge(s_free[k], v)
                    gather(k, TILES)
            pool.wait_ge(s_free[0], GROUPS // 2 - 1)
            gather(0, TILES)
            pool.wait_ge(s_free[1], GROUPS // 2 - 1)
            gather(1, 2 * TAILC)

            pool.wait_ge(s_flag, 1)
            f = pool.value_load(flag[0:1, 0:1], min_val=0, max_val=P)
            with pool.If(f > 0):
                with pool.Fori(1, E // SLOW + 1) as v:
                    pool.wait_ge(s_ix, 32)
                    pool.wait_ge(s_fin, v)
                    pool.indirect_dma_start(
                        out=slow_raw[:, :], out_offset=None, in_=x,
                        in_offset=bass.IndirectOffsetOnAxis(ap=slow_idx[:, 0:1], axis=0)).then_inc(s_fg, 16)

        @block.scalar
        def _(act):
            act.dma_start(w[:, :], packed).then_inc(s_w, 16)
            act.wait_ge(s_zero, 1)
            for c0 in range(ZSPLIT, AGGW, NODES):
                n = min(NODES, AGGW - c0)
                last = act.activation(node_in[0:H, c0:c0 + n], zeros[:, 0:n], ACT.Copy)
            last.then_inc(s_zeroa, 1)
            for n in range(TABS):
                k, q = divmod(n, TABK)
                act.wait_ge(s_tabp, n + 1)
                tab = (src_tab, dst_tab)[k]
                b0, b1 = 2 * q, min(2 * q + 2, CBLK)
                act.activation(tab[:, b0 * P:b1 * P, :].rearrange("p (b c) t -> p b t c", c=P),
                               ps_tab[n % 7][:, 0:(b1 - b0) * 2 * P].rearrange("p (b t c) -> p b t c", t=2, c=P),
                               ACT.Copy).then_inc(s_tabc, 1)

            def edge_iter(i, k, opens, mid, late, nodes, after):
                if mid:
                    act.wait_ge(s_l2, i)
                    act.activation(h2[:, :], ps_l2[:, :], ACT.Relu, bias=bias1[:, 2:3]).then_inc(s_h2, 1)
                if opens:
                    act.wait_ge(s_tra, i + 1)
                    act.activation(xT[:, 0:GROUP // 2], ps_ta[:, :], ACT.Copy).then_inc(s_xa, 1)
                if late:
                    act.wait_ge(s_rd, i - 1)
                    for q in range(TILES):
                        last = act.activation(cen[:, k, q, 0:H - 1], ps_t2[k][:, q * H:(q + 1) * H - 1], ACT.Identity,
                                              scale=rstd[:, 1 - k, OUT_T + q:OUT_T + q + 1], bias=shift[:, 1 - k, q:q + 1])
                    last.then_inc(s_cen, 1)
                if opens:
                    act.wait_ge(s_l0, i + 1)
                    act.activation(h0[:, :], ps_l0[:, :], ACT.Relu, bias=bias1[:, 0:1]).then_inc(s_h0, 1)
                if opens or mid:
                    act.wait_ge(s_var, i + 2)
                    root_step(P, *span(i)).then_inc(s_root, 1)
                if after:
                    act.wait_ge(s_trb, i + 2)
                    act.activation(xT[:, GROUP // 2:GROUP], ps_tb[:, :], ACT.Copy).then_inc(s_xb, 1)
                if nodes is not None:
                    act.wait_ge(s_hT, i - T0)
                    act.activation(node_in[H:P, bass.ds(nodes * NODES, NODES)].rearrange("d (p t) -> d t p", t=HALF),
                                   ps_agg[H:P, :].rearrange("d (t p) -> d t p", p=P), ACT.Copy).then_inc(s_hTc, 1)
                if opens:
                    act.wait_ge(s_l1, i + 1)
                    act.activation(h1[:, :], ps_l1[:, :], ACT.Relu, bias=bias1[:, 1:2]).then_inc(s_h1, 1)

            act.wait_ge(s_w, 16)
            act.wait_ge(s_var, 1)
            root_step(P, RAW_T, OUT_T).then_inc(s_root, 1)
            act.wait_ge(s_trb, 1)
            act.activation(xT[:, GROUP // 2:GROUP], ps_tb[:, :], ACT.Copy).then_inc(s_xb, 1)
            edge_iter(0, 0, True, False, 0, None, True)
            edge_iter(1, 1, True, True, 0, None, True)
            for i in (2, 3, 4):
                edge_iter(i, i % 2, True, True, 1, None, True)
            with act.Fori(2, NBE // 2 + 2) as n:
                edge_iter(n * 2 + 1, 1, True, True, 1, n * 2 - 4, True)
                edge_iter(n * 2 + 2, 0, True, True, 1, n * 2 - 3, True)
            act.wait_ge(s_flagp, 1)
            act.activation(flag[0:1, 0:1], ps_agg[H:H + 1, 0:1], ACT.Copy).then_inc(s_flag, 1)
            with act.Fori(NBE // 2 + 2, GROUPS // 2 - 2) as n:
                edge_iter(n * 2 + 1, 1, True, True, 1, None, True)
                edge_iter(n * 2 + 2, 0, True, True, 1, None, True)
            edge_iter(GROUPS - 3, 1, True, True, 1, None, True)
            edge_iter(GROUPS - 2, 0, True, True, 1, None, True)
            edge_iter(GROUPS - 1, 1, True, True, 1, None, False)
            edge_iter(GROUPS, 0, False, True, 1, None, False)
            edge_iter(GROUPS + 1, 1, False, False, 1, None, False)

            act.wait_ge(s_flag, 1)
            f = act.value_load(flag[0:1, 0:1], min_val=0, max_val=P)
            with act.If(f > 0):
                with act.Fori(1, E // SLOW + 1) as v:
                    act.wait_ge(s_fvar, v * 2 - 1)
                    root_step(SLOW, 0, 1).then_inc(s_froot, 1)
                    act.wait_ge(s_fT, v)
                    act.activation(xT[:, 0:SLOW], ps_ta[:, 0:SLOW], ACT.Copy).then_inc(s_fx, 1)
                    for k, (ps, h) in enumerate(((ps_l0, h0), (ps_l1, h1), (ps_l2, h2))):
                        act.wait_ge(s_fl[k], v)
                        act.activation(h[0:H, 0:SLOW], ps[0:H, 0:SLOW], ACT.Relu, bias=bias1[0:H, k:k + 1]).then_inc(s_fh[k], 1)
                    act.wait_ge(s_fvar, v * 2)
                    root_step(SLOW, 0, 1).then_inc(s_froot, 1)

            act.wait_ge(s_wc, WC)
            for q in range(PAIRS + 1):
                if q < PAIRS:
                    act.wait_ge(s_n0, q + 1)
                    if q:
                        act.wait_ge(s_n1, q)
                    act.activation(h0[:, :], ps_l0[:, :], ACT.Relu, bias=bias2[:, 0:1]).then_inc(s_nh0, 1)
                if q:
                    act.wait_ge(s_n2, q)
                    if q > 1:
                        act.wait_ge(s_no, q - 1)
                    act.activation(h2[:, :], ps_l2[:, :], ACT.Relu, bias=bias2[:, 2:3]).then_inc(s_nh2, 1)
                if q < PAIRS:
                    act.wait_ge(s_n1, q + 1)
                    if q:
                        act.wait_ge(s_n2, q)
                    act.activation(h1[:, :], ps_l1[:, :], ACT.Relu, bias=bias2[:, 1:2]).then_inc(s_nh1, 1)
                if q:
                    act.wait_ge(s_nvar, q)
                    root_step(P, 0, TILES).then_inc(s_nroot, 1)

        @block.vector
        def _(dve):
            dve.memset(zeros[:, :], 0.0)
            dve.memset(base_row[:, :], 0).then_inc(s_zero, 1)
            dve.memset(xn[:, (NBLK - 1) * HALF:NBE * HALF, :], 0.0).then_inc(s_zero, 1)
            dve.memset(node_in[0:H, 0:ZSPLIT], 0.0)
            dve.memset(wno[:, :], 0.0)
            dve.memset(cen[:, :, :, H - 1], 1.0).then_inc(s_zero, 1)
            chain = [0]

            def link(ins):
                chain[0] += 1
                ins.then_inc(s_dve, 1)
                dve.wait_ge(s_dve, chain[0])

            dve.wait_ge(s_nats, 16 * NATS)
            nc.vector.tensor_copy(natf[:, 0, :, :], nat[:, 0, :, :]).then_inc(s_natf, 1)
            dve.wait_ge(s_natd, 16 * NATS)
            link(nc.vector.tensor_copy(natf[:, 1, :, :], nat[:, 1, :, :]))
            link(nc.vector.tensor_scalar(base_f[:, :], natf[:, 1, :, 0], 0.0, None, ALU.max))
            nc.vector.tensor_tensor(natf[:, 1, :, :], natf[:, 1, :, :],
                                    base_f[:, :].unsqueeze(2).to_broadcast([P, CBLK, CHUNK]),
                                    ALU.subtract).then_inc(s_natf, 1)

            dve.wait_ge(s_w, 16)
            dve.wait_ge(s_const, 1)
            link(nc.vector.tensor_scalar(lnw[:, 0, :], drop63[:, :], col[:, 0:1], None, ALU.mult))
            nc.vector.tensor_copy(lnw[:, 0, H - 1:H], col[:, 1:2]).then_inc(s_wc, 1)
            dve.wait_ge(s_wp, 1)
            link(nc.vector.tensor_copy(lnw[:, 1, :], ps_agg[0:H, 0:H]))
            nc.vector.tensor_tensor(lnw[:, 1, H - 1:H], lnw[:, 1, H - 1:H], col[:, 2:3], ALU.add).then_inc(s_wc, 1)
            dve.wait_ge(s_wp, 2)
            nc.vector.tensor_copy(wn0[0:H, :], ps_agg[0:H, 64:64 + H])
            nc.vector.tensor_tensor(bias2[0:H, 0:1], bias2[0:H, 0:1], ps_agg[0:H, 128:129], ALU.add)
            nc.vector.tensor_tensor(bias2[H:P, 0:1], bias2[H:P, 0:1], ps_agg[H:P, 128:129], ALU.add)
            link(nc.vector.tensor_tensor(bo_row[:, :], bo_row[:, :], ps_agg[0:1, 256:256 + H], ALU.add))
            nc.vector.tensor_scalar(w2o_s[:, :], w2o_s[:, :], col[:, 4:5], None, ALU.mult).then_inc(s_wc, 1)
            dve.wait_ge(s_wp, 3)
            nc.vector.tensor_copy(wno[0:H, 0:H], ps_agg[0:H, 320:320 + H])
            nc.vector.tensor_copy(wno[H:P, H:P], ps_agg[H:P, 320:320 + H])
            nc.vector.tensor_copy(bo_all[:, :], ps_agg[:, 384:384 + H]).then_inc(s_wc, 1)

            dve.wait_ge(s_natf, 2)
            d = natf[:, 1, :, :].rearrange("p b e -> p (b e)")
            real = nat[:, 1, :, :].rearrange("p b e -> p (b e)").bitcast(f32)
            nc.vector.tensor_reduce(bad[:, 0:1], d, AX.X, ALU.max)
            link(nc.vector.scalar_tensor_tensor(real, d, PAD / 2, d, ALU.is_gt, ALU.mult))
            link(nc.vector.tensor_reduce(bad[:, 1:2], real, AX.X, ALU.min))
            link(nc.vector.tensor_scalar(bad[:, 2:3], bad[:, 0:1], float(WIN - 1), None, ALU.is_gt))
            nc.vector.scalar_tensor_tensor(bad[:, 2:3], bad[:, 1:2], 0.0, bad[:, 2:3],
                                           ALU.is_lt, ALU.add).then_inc(s_bad, 1)

            base_regs = [dve.alloc_register(f"window_base{c}") for c in range(CPG)]

            def edge_iter(i, k, gathered, stage, mid, agg, nodes):
                step = [0]

                def link(ins):
                    step[0] += 1
                    ins.then_inc(s_st, 1)
                    dve.wait_ge(s_st, i * 8 + 8 + step[0])

                j = 1 - k
                lo, hi = span(i)
                if agg:
                    a = i - 2
                    dve.reg_load(base_regs, base_row[0:1, bass.ds(a * CPG, CPG)])
                    bases = [dve.snap(reg, min_val=0, max_val=N - 1) for reg in base_regs]
                if gathered is not None:
                    dve.wait_ge(s_gath[j], gathered)
                    for q in range(TILES):
                        last = nc.vector.bn_stats(bn[:, RAW_T + q, :], raw[:, j, q, :])
                if nodes is not None:
                    xb = xn[:, bass.ds(nodes * HALF, HALF), :]
                    for q in range(HALF):
                        last = nc.vector.bn_stats(bn[:, NODE_T + q, :], xb[:, q, :])
                if mid:
                    dve.wait_ge(s_t2, i)
                    ps = ps_t2[j][:, :].rearrange("p (q d) -> p q d", d=H)
                    for q in range(TILES):
                        last = nc.vector.bn_stats(bn[:, OUT_T + q, :], ps[:, q, :])
                if gathered is not None or mid:
                    link(last)
                    mean_steps(link, P, lo, hi)
                    var_step(P, lo, hi).then_inc(s_var, 1)
                if stage:
                    nc.vector.tensor_copy(idx[:, j, :], src_tab[:, bass.ds(i * CPG + 3 * CPG, CPG), :]
                                          .rearrange("p c t -> p (c t)"))
                if gathered is not None:
                    nc.vector.tensor_tensor(rows[:, j, 0, :, :], raw[:, j, :, :],
                                            st[:, 1, RAW_T:OUT_T].unsqueeze(2).to_broadcast([P, TILES, H]),
                                            ALU.subtract).then_inc(s_free[j], 1)
                if nodes is not None:
                    nc.vector.tensor_tensor(hs[:, k, :, :], xb, st[:, 1, NODE_T:RAW_T].unsqueeze(2)
                                            .to_broadcast([P, HALF, H]), ALU.subtract)
                if mid:
                    nc.vector.tensor_tensor(
                        onehot[:, j, :, :], iota[:, :].unsqueeze(1).to_broadcast([P, TILES, WIN]),
                        dst_tab[:, bass.ds(i * CPG - CPG, CPG), :].rearrange("p c t -> p (c t)").unsqueeze(2)
                        .to_broadcast([P, TILES, WIN]), ALU.is_equal).then_inc(s_oh, 1)
                if agg:
                    dve.wait_ge(s_agg, i - 1)
                    for c in range(CPG):
                        if agg > 1 or c:
                            dve.wait_ge(s_add, a * CPG + c)
                        win = node_in[0:H, bass.ds(bases[c], WIN)]
                        nc.vector.tensor_tensor(win, win, ps_agg[0:H, k * AW + c * WIN:k * AW + (c + 1) * WIN],
                                                ALU.add).then_inc(s_add, 1)
                if gathered is not None or mid:
                    dve.wait_ge(s_root, i + 2)
                    rstd_steps(link, P, lo, hi, k)
                if mid:
                    nc.vector.scalar_tensor_tensor(shift[:, k, :], st[:, 1, OUT_T:ALLT], -1.0, rstd[:, k, OUT_T:ALLT],
                                                   ALU.mult, ALU.mult).then_inc(s_rd, 1)
                if gathered is not None:
                    nc.vector.scalar_tensor_tensor(rows[:, j, 0, :, :], rows[:, j, 0, :, :], 0.0,
                                                   rstd[:, k, RAW_T:OUT_T].unsqueeze(2).to_broadcast([P, TILES, H]),
                                                   ALU.max, ALU.mult).then_inc(s_norm, 1)
                if nodes is not None:
                    nc.vector.scalar_tensor_tensor(hs[:, k, :, :], hs[:, k, :, :], 0.0,
                                                   rstd[:, k, NODE_T:RAW_T].unsqueeze(2).to_broadcast([P, HALF, H]),
                                                   ALU.max, ALU.mult).then_inc(s_ln, 1)
                    nc.vector.tensor_tensor(xb, xb, bo_all[:, :].unsqueeze(1).to_broadcast([P, HALF, H]),
                                            ALU.add).then_inc(s_xs, 1)
                    dve.wait_ge(s_xs, i * 2 + 1 - 2 * T0)
                    nc.vector.tensor_tensor(xb, xb, hs[:, k, :, :], ALU.add).then_inc(s_xs, 1)

            GV = 16 * TILES
            dve.wait_ge(s_tabc, TABK)
            edge_iter(-1, 1, GV, True, False, 0, None)
            edge_iter(0, 0, GV, True, False, 0, None)
            edge_iter(1, 1, 2 * GV, True, True, 0, None)
            dve.wait_ge(s_zero, 3)
            dve.wait_ge(s_zeroa, 1)
            dve.wait_ge(s_base, 16)
            edge_iter(2, 0, 2 * GV, True, True, 1, None)
            edge_iter(3, 1, 3 * GV, True, True, 2, None)
            dve.wait_ge(s_x, 32)
            with dve.Fori(2, NBE // 2 + 2) as n:
                edge_iter(n * 2, 0, n * GV + GV, True, True, 2, n * 2 - 4)
                edge_iter(n * 2 + 1, 1, n * GV + 2 * GV, True, True, 2, n * 2 - 3)
            with dve.Fori(NBE // 2 + 2, GROUPS // 2 - 2) as n:
                edge_iter(n * 2, 0, n * GV + GV, True, True, 2, None)
                edge_iter(n * 2 + 1, 1, n * GV + 2 * GV, True, True, 2, None)
            n = GROUPS // 2
            edge_iter(GROUPS - 4, 0, (n - 1) * GV, True, True, 2, None)
            edge_iter(GROUPS - 3, 1, n * GV, False, True, 2, None)
            edge_iter(GROUPS - 2, 0, (n - 1) * GV + 32 * TAILC, False, True, 2, None)
            edge_iter(GROUPS - 1, 1, None, False, True, 2, None)
            edge_iter(GROUPS, 0, None, False, True, 2, None)
            edge_iter(GROUPS + 1, 1, None, False, False, 2, None)

            dve.wait_ge(s_flag, 1)
            dve.wait_ge(s_add, CHUNKS)
            f = dve.value_load(flag[0:1, 0:1], min_val=0, max_val=P)
            with dve.If(f > 0):
                dve.memset(node_in[0:H, :], 0.0).then_inc(s_fz, 1)
                dve.wait_ge(s_fz, 1)
                dve.sem_inc(s_fd, 1)
                dve.sem_inc(s_fadd, 1)
                with dve.Fori(1, E // SLOW + 1) as v:
                    step = [0]

                    def link(ins):
                        step[0] += 1
                        ins.then_inc(s_fs, 1)
                        dve.wait_ge(s_fs, v * 16 - 16 + step[0])

                    dve.wait_ge(s_fg, v * 16)
                    link(nc.vector.bn_stats(bn[0:SLOW, 0, :], slow_raw[:, :]))
                    mean_steps(link, SLOW, 0, 1)
                    nc.vector.tensor_scalar(slow_rows[:, 0, :], slow_raw[:, :], st[0:SLOW, 1, 0:1], None, ALU.subtract)
                    var_step(SLOW, 0, 1).then_inc(s_fvar, 1)
                    dve.wait_ge(s_froot, v * 2 - 1)
                    rstd_steps(link, SLOW, 0, 1, 0)
                    nc.vector.tensor_scalar(slow_rows[:, 0, :], slow_rows[:, 0, :], 0.0, rstd[0:SLOW, 0, 0:1],
                                            ALU.max, ALU.mult).then_inc(s_frow, 1)
                    dve.wait_ge(s_fU, v)
                    link(nc.vector.bn_stats(bn[0:SLOW, 0, :], ps_t2[0][0:SLOW, 0:H]))
                    mean_steps(link, SLOW, 0, 1)
                    nc.vector.tensor_scalar(slow_cen[:, :], ps_t2[0][0:SLOW, 0:H], st[0:SLOW, 1, 0:1], None, ALU.subtract)
                    var_step(SLOW, 0, 1).then_inc(s_fvar, 1)
                    dve.wait_ge(s_froot, v * 2)
                    rstd_steps(link, SLOW, 0, 1, 0)
                    nc.vector.scalar_tensor_tensor(slow_cen[:, H - 1:H], st[0:SLOW, 4, 0:1], EPS,
                                                   rstd[0:SLOW, 0, 0:1], ALU.add, ALU.mult)
                    nc.vector.tensor_scalar(slow_diag[:, :], ident[0:SLOW, 0:SLOW], rstd[0:SLOW, 0, 0:1],
                                            None, ALU.mult).then_inc(s_frd, 1)
                    dve.wait_ge(s_fm, v)
                    nc.vector.tensor_copy(slow_msg[:, :], ps_tb[0:H, 0:SLOW]).then_inc(s_fc, 1)
                    dve.wait_ge(s_fz, 1)
                    dve.wait_ge(s_fc, v)
                    with dve.Fori(0, SLOW) as e:
                        node = dve.value_load(slow_dst[0:1, bass.ds(e, 1)], min_val=0, max_val=N - 1)
                        dve.wait_ge(s_fadd, v * SLOW + e - (SLOW - 1))
                        c = node_in[0:H, bass.ds(node, 1)]
                        nc.vector.tensor_tensor(c, c, slow_msg[:, bass.ds(e, 1)], ALU.add).then_inc(s_fadd, 1)
                    dve.wait_ge(s_fadd, v * SLOW + 1)
                    dve.sem_inc(s_fd, 1)
            dve.sem_inc(s_sums, 1)

            dve.wait_ge(s_xs, 2 * NBE)
            for q in range(PAIRS):
                step = [0]

                def link(ins):
                    step[0] += 1
                    ins.then_inc(s_nst, 1)
                    dve.wait_ge(s_nst, q * 8 + step[0])

                dve.wait_ge(s_nt, q + 1)
                ps = ps_t2[0][:, :].rearrange("p (k h d) -> p (k h) d", h=2, d=H)
                for t in range(TILES):
                    last = nc.vector.bn_stats(bn[:, t, :], ps[:, t, :])
                link(last)
                mean_steps(link, P, 0, TILES)
                var_step(P, 0, TILES).then_inc(s_nvar, 1)
                if q:
                    dve.wait_ge(s_nres, q)
                dve.wait_ge(s_nroot, q + 1)
                rstd_steps(link, P, 0, TILES, 0)
                dve.wait_ge(s_no, q + 1)
                if q >= 2:
                    dve.wait_ge(s_out[q % 2], 16 * (q // 2))
                po = (ps_ta, ps_tb)[q % 2][:, :].rearrange("p (k h d) -> p k h d", h=2, d=H)
                halves = min(2, NBLK - 2 * q)
                for t in range(HALF):
                    for h in range(halves):
                        j = t * 2 + h
                        last = nc.vector.scalar_tensor_tensor(
                            res[:, q % 2, h * HALF + t, :], po[:, t, h, :], rstd[:, 0, j:j + 1],
                            xn[:, (2 * q + h) * HALF + t, :], ALU.mult, ALU.add)
                last.then_inc(s_nres, 1)

        @block.tensor
        def _(pe):
            pe.wait_ge(s_const, 1)
            for n in range(TABS):
                k, q = divmod(n, TABK)
                if q == 0:
                    pe.wait_ge(s_natf, k + 1)
                if n >= 7:
                    pe.wait_ge(s_tabc, n - 6)
                for b in range(2 * q, min(2 * q + 2, CBLK)):
                    for t in range(2):
                        o = (b - 2 * q) * 2 * P + t * P
                        last = pe.transpose(ps_tab[n % 7][:, o:o + P],
                                            natf[:, k, b, :].rearrange("c (p t) -> c t p", t=2)[:, t, :], ident[:, :])
                last.then_inc(s_tabp, 1)
            pe.wait_ge(s_w, 16)
            pe.wait_ge(s_wc, 1)
            pe.matmul(ps_agg[0:H, 0:H], w1o_s[:, :], lnw[:, 0, :], start=True, stop=True).then_inc(s_wp, 1)
            pe.wait_ge(s_wc, 2)
            pe.matmul(ps_agg[0:H, 64:64 + H], lnw[:, 1, :], w2a_s[:, :], start=True, stop=True)
            pe.matmul(ps_agg[0:H, 128:129], w2u_s[:, :], col[:, 3:4], start=True, stop=True)
            pe.matmul(ps_agg[H:P, 128:129], w2u_s[:, :], col[:, 3:4], start=True, stop=True)
            pe.matmul(ps_agg[0:1, 256:256 + H], col[:, 5:6], w2o_s[:, :], start=True, stop=True).then_inc(s_wp, 1)
            pe.wait_ge(s_wc, 3)
            pe.matmul(ps_agg[0:H, 320:320 + H], lnw[:, 2, :], w2o_s[:, :], start=True, stop=True)
            pe.matmul(ps_agg[H:P, 320:320 + H], lnw[:, 2, :], w2o_s[:, :], start=True, stop=True)
            pe.matmul(ps_agg[:, 384:384 + H], one_row[:, :], bo_row[:, :], start=True, stop=True).then_inc(s_wp, 1)
            pe.wait_ge(s_wc, WC)
            pe.wait_ge(s_tabc, TABS)

            def attrs_turned(k, attrs):
                pe.wait_ge(s_attr[k], attrs)
                for c in range(CPG):
                    last = pe.transpose(ps_tb[:, c * P:(c + 1) * P],
                                        rows[:, k, 1, 2 * c:2 * c + 2, :].rearrange("p t d -> p (t d)"), ident[:, :])
                last.then_inc(s_trb, 1)

            def edge_iter(i, k, opens, mid, agg, attrs, nodes):
                if mid:
                    pe.wait_ge(s_h1, i)
                    pe.matmul(ps_l2[:, :], wl2[:, :], h1[:, :], start=True, stop=True).then_inc(s_l2, 1)
                if opens:
                    pe.wait_ge(s_norm, i + 1)
                    for c in range(CPG):
                        last = pe.transpose(ps_ta[:, c * P:(c + 1) * P],
                                            rows[:, k, 0, 2 * c:2 * c + 2, :].rearrange("p t d -> p (t d)"), ident[:, :])
                    last.then_inc(s_tra, 1)
                if mid:
                    pe.wait_ge(s_h2, i)
                    for t in range(HALF):
                        last = pe.transpose(ps_t2[1 - k][:, t * P:(t + 1) * P], h2[:, t * P:(t + 1) * P], ident[:, :])
                    last.then_inc(s_t2, 1)
                if opens:
                    pe.wait_ge(s_xb, i + 1)
                    pe.matmul(ps_l0[:, :], wl0e[:, :], xT[:, GROUP // 2:GROUP], start=True, stop=False)
                    pe.wait_ge(s_xa, i + 1)
                    pe.matmul(ps_l0[:, :], wl0h[:, :], xT[:, 0:GROUP // 2], start=False, stop=True).then_inc(s_l0, 1)
                if attrs is not None:
                    attrs_turned(1 - k, attrs)
                if agg:
                    pe.wait_ge(s_cen, i - 1)
                    pe.wait_ge(s_oh, i - 1)
                    for c in range(CPG):
                        for t in range(2):
                            o = k * AW + c * WIN
                            last = pe.matmul(ps_agg[0:H, o:o + WIN], cen[:, k, 2 * c + t, :],
                                             onehot[:, k, 2 * c + t, :], start=(t == 0), stop=(t == 1))
                    last.then_inc(s_agg, 1)
                if nodes:
                    pe.wait_ge(s_ln, i - T0)
                    for t in range(HALF):
                        last = pe.matmul(ps_agg[H:P, t * P:(t + 1) * P], hs[:, 1 - k, t, :], ident[:, :],
                                         start=True, stop=True)
                    last.then_inc(s_hT, 1)
                if opens:
                    pe.wait_ge(s_h0, i + 1)
                    pe.matmul(ps_l1[:, :], wl1[:, :], h0[:, :], start=True, stop=True).then_inc(s_l1, 1)

            attrs_turned(0, 16)
            edge_iter(0, 0, True, False, False, 16, False)
            edge_iter(1, 1, True, True, False, 32, False)
            for i in (2, 3, 4):
                edge_iter(i, i % 2, True, True, True, 16 * ((i + 1) // 2 + 1), False)
            with pe.Fori(2, NBE // 2 + 2) as n:
                edge_iter(n * 2 + 1, 1, True, True, True, n * 16 + 32, True)
                edge_iter(n * 2 + 2, 0, True, True, True, n * 16 + 32, True)
            pe.wait_ge(s_bad, 1)
            pe.wait_ge(s_hTc, NBE)
            pe.matmul(ps_agg[H:H + 1, 0:1], bad[:, 2:3], ones[:, :], start=True, stop=True).then_inc(s_flagp, 1)
            with pe.Fori(NBE // 2 + 2, GROUPS // 2 - 2) as n:
                edge_iter(n * 2 + 1, 1, True, True, True, n * 16 + 32, False)
                edge_iter(n * 2 + 2, 0, True, True, True, n * 16 + 32, False)
            n = GROUPS // 2
            edge_iter(GROUPS - 3, 1, True, True, True, n * 16, False)
            edge_iter(GROUPS - 2, 0, True, True, True, n * 16 - 16 + 16 * TAILC, False)
            edge_iter(GROUPS - 1, 1, True, True, True, None, False)
            edge_iter(GROUPS, 0, False, True, True, None, False)
            edge_iter(GROUPS + 1, 1, False, False, True, None, False)

            pe.wait_ge(s_flag, 1)
            f = pe.value_load(flag[0:1, 0:1], min_val=0, max_val=P)
            with pe.If(f > 0):
                with pe.Fori(1, E // SLOW + 1) as v:
                    pe.wait_ge(s_fz, 1)
                    pe.wait_ge(s_frow, v)
                    pe.transpose(ps_ta[:, 0:SLOW], slow_rows[:, :, :].rearrange("p k d -> p (k d)"),
                                 ident[0:SLOW, 0:SLOW]).then_inc(s_fT, 1)
                    pe.wait_ge(s_fz, 1)
                    pe.wait_ge(s_fx, v)
                    pe.matmul(ps_l0[0:H, 0:SLOW], wl0[:, :], xT[:, 0:SLOW], start=True, stop=True).then_inc(s_fl[0], 1)
                    for k, (ps, w, h) in enumerate(((ps_l1, wl1, h0), (ps_l2, wl2, h1))):
                        pe.wait_ge(s_fz, 1)
                        pe.wait_ge(s_fh[k], v)
                        pe.matmul(ps[0:H, 0:SLOW], w[0:H, 0:H], h[0:H, 0:SLOW], start=True, stop=True).then_inc(s_fl[k + 1], 1)
                    pe.wait_ge(s_fz, 1)
                    pe.wait_ge(s_fh[2], v)
                    pe.transpose(ps_t2[0][0:SLOW, 0:H], h2[0:H, 0:SLOW], ident[0:H, 0:H]).then_inc(s_fU, 1)
                    pe.wait_ge(s_fz, 1)
                    pe.wait_ge(s_frd, v)
                    pe.matmul(ps_tb[0:H, 0:SLOW], slow_cen[:, :], slow_diag[:, :], start=True, stop=True).then_inc(s_fm, 1)

            pe.wait_ge(s_sums, 1)
            hv = h2[:, :].rearrange("d (p t) -> d t p", t=HALF)
            for q in range(PAIRS + 1):
                if q < PAIRS:
                    c0 = 2 * q * NODES
                    if q:
                        pe.wait_ge(s_nh0, q)
                    for h in range(2):
                        last = pe.matmul(ps_l0[h * H:(h + 1) * H, :], wn0[:, :],
                                         node_in[:, c0 + h * NODES:c0 + (h + 1) * NODES], start=True, stop=True)
                    last.then_inc(s_n0, 1)
                if q:
                    pe.wait_ge(s_nh1, q)
                    if q > 1:
                        pe.wait_ge(s_nh2, q - 1)
                    pe.matmul(ps_l2[:, :], wn2[:, :], h1[:, :], start=True, stop=True).then_inc(s_n2, 1)
                if q < PAIRS:
                    pe.wait_ge(s_nh0, q + 1)
                    if q:
                        pe.wait_ge(s_nh1, q)
                    pe.matmul(ps_l1[:, :], wn1[:, :], h0[:, :], start=True, stop=True).then_inc(s_n1, 1)
                if q:
                    pe.wait_ge(s_nh2, q)
                    if q > 1:
                        pe.wait_ge(s_nvar, q - 1)
                    for t in range(HALF):
                        last = pe.transpose(ps_t2[0][:, t * P:(t + 1) * P], hv[:, t, :], ident[:, :])
                    last.then_inc(s_nt, 1)
                    if q > 2:
                        pe.wait_ge(s_nres, q - 2)
                    for t in range(HALF):
                        last = pe.matmul((ps_ta, ps_tb)[(q - 1) % 2][:, t * P:(t + 1) * P], hv[:, t, :], wno[:, :],
                                         start=True, stop=True)
                    last.then_inc(s_no, 1)


def pack_weights(wt):
    import numpy as _np
    at, cols = weight_columns()
    packed = _np.zeros((128, cols), _np.float32)

    def place(name, row, a, col=0):
        a = a.reshape(a.shape[0], -1)
        c = at[name][0] + col
        packed[row:row + a.shape[0], c:c + a.shape[1]] = a

    w1_0, w2_0 = wt["w1_0"], wt["w2_0"]
    for lo in (0, 64):
        for name, a in (("l0h", w1_0[:64]), ("l0e", w1_0[64:]), ("l1", wt["w1_1"]), ("l2", wt["w1_2"]),
                        ("n1", wt["w2_1"]), ("n2", wt["w2_2"])):
            place(name, lo, a, lo)
        for k in range(3):
            place("bias1", lo, wt[f"b1_{k}"], k)
            place("bias2", lo, wt[f"b2_{k}"], k)
    place("l0", 0, w1_0)
    place("n0", 64, w2_0[:64])
    place("w2a", 0, w2_0[64:128])
    place("w2u", 0, w2_0[128:])
    place("w1o", 0, wt["w1_o"])
    place("w2o", 0, wt["w2_o"])
    for k, a in enumerate((wt["g1"], wt["be1"], wt["b1_o"], wt["u"][0], wt["g2"], wt["be2"])):
        place("col", 0, a, k)
    place("bo", 0, wt["b2_o"].reshape(1, 64))
    return packed


def kernel(**inputs):
    import numpy as _np
    import concourse.bacc as _bacc
    from concourse import mybir as _mybir
    from concourse.bass_utils import run_bass_kernel_spmd as _run

    nc = _bacc.Bacc("TRN2", target_bir_lowering=False, num_devices=1)
    arrays, args = {}, []
    given = {"x": inputs["x"], "src": inputs["src"], "dst": inputs["dst"], "edge_attr": inputs["edge_attr_64"],
             "weights": pack_weights({n[7:]: _np.asarray(a) for n, a in inputs.items() if n.startswith("L0_gnn_")})}
    for name, a in given.items():
        a = _np.ascontiguousarray(a)
        arrays[f"in_{name}_dram"] = a
        args.append(nc.dram_tensor(f"in_{name}_dram", a.shape, _mybir.dt.from_np(a.dtype), kind="ExternalInput").ap())
    shape = tuple(inputs['x'].shape)
    out = nc.dram_tensor("out_0_dram", shape, _mybir.dt.float32, kind="ExternalOutput").ap()
    gnn_layer(nc, *args, out)
    r = _run(nc, [arrays], core_ids=[0])
    return r.results[0]["out_0_dram"]
```

```python
import concourse.bass as bass
from concourse import mybir
from contextlib import ExitStack


def weight_columns():
    at, c = {}, 0
    for name, n in (("l0h", 128), ("l0e", 128), ("l1", 128), ("l2", 128), ("bias1", 3), ("n1", 128), ("n2", 128),
                    ("l0", 64), ("n0", 64), ("w1o", 64), ("w2a", 64), ("w2u", 64), ("w2o", 64), ("bias2", 3),
                    ("col", 6), ("bo", 64)):
        at[name] = (c, n)
        c += n
    return at, c


def gnn_layer(nc, x, src, dst, edge_attr, packed, out):
    f32, i32 = mybir.dt.float32, mybir.dt.int32
    ALU, ACT, AX = mybir.AluOpType, mybir.ActivationFunctionType, mybir.AxisListType

    P = 128
    N, H = x.shape
    E = src.shape[0]
    EPS = 1e-5
    TILES = 8
    HALF = TILES // 2
    GROUP = TILES * P
    CHUNK = 2 * P
    CPG = GROUP // CHUNK
    WIN = 64
    GROUPS = 2 * -(-E // (2 * GROUP))
    FULL = E // GROUP
    assert FULL == GROUPS - 1 and E % 2 == 0 and GROUPS >= 6
    CHUNKS = GROUPS * CPG
    CBLK = -(-CHUNKS // P)
    NODES = HALF * P
    NBLK = -(-N // NODES)
    LASTP = (N - (NBLK - 1) * NODES) // HALF
    assert (N - (NBLK - 1) * NODES) % HALF == 0 and NBLK > 1
    PAIRS = -(-NBLK // 2)
    NBE = 2 * PAIRS
    AGGW = NBE * NODES + WIN
    NPT = HALF // 2
    PARTS = 2 * NBE
    T0 = 4
    assert GROUPS > PARTS + 9
    PAD = -float(1 << 22)
    SLOW = 64
    assert E % SLOW == 0

    REALC = -(-E // CHUNK)
    TAILC = REALC - FULL * CPG
    TABK = -(-CBLK // 2)
    TABS = 2 * TABK
    NATS = sum(1 for n in (E // (P * CHUNK), E % (P * CHUNK) // CHUNK, E % CHUNK) if n)
    WC = 4
    XSTEP = -(-(NBLK - 1) // 6)
    XPIECES = [(b, min(b + XSTEP, NBLK - 1)) for b in range(0, NBLK - 1, XSTEP)]
    AT, COLS = weight_columns()
    ALLT = NPT + 2 * TILES
    NODE_T, RAW_T, OUT_T = 0, NPT, NPT + TILES
    ZSPLIT = AGGW * 2 // 5 // 64 * 64
    OUTS = [sum(16 * ((min(2 * q + 2, NBLK) - 2 * q > (2 * q + 2 >= NBLK)) + (2 * q + 2 >= NBLK))
                for q in range(PAIRS) if q % 2 == k) for k in range(2)]

    ctx = ExitStack()
    with ctx:
        def sb(name, shape, dt=f32):
            return ctx.enter_context(nc.sbuf_tensor(name, shape, dt))

        def sem(name):
            return ctx.enter_context(nc.semaphore(name))

        node_in = sb("node_in", [P, AGGW])
        xn = sb("xn", [P, NBE * HALF, H])
        hs = sb("hs", [P, 2, NPT, H])
        nat = sb("nat", [P, 2, CBLK, CHUNK], i32)
        natf = sb("natf", [P, 2, CBLK, CHUNK])
        base_f = sb("base_f", [P, CBLK])
        src_tab = sb("src_tab", [P, CBLK * P, 2], i32)
        dst_tab = sb("dst_tab", [P, CBLK * P, 2])
        base_row = sb("base_row", [1, CHUNKS], i32)
        rows = sb("rows", [P, 2, 2, TILES, H])
        raw = sb("raw", [P, 2, TILES, H])
        idx = sb("idx", [P, 2, TILES], i32)
        xT = sb("xT", [P, GROUP])
        h0 = sb("h0", [P, NODES])
        h1 = sb("h1", [P, NODES])
        h2 = sb("h2", [P, NODES])
        cen = sb("cen", [P, 2, TILES, H])
        onehot = sb("onehot", [P, 2, TILES, WIN])
        bn = sb("bn", [P, ALLT, 6])
        st = sb("st", [P, 7, ALLT])
        rstd = sb("rstd", [P, 2, ALLT])
        shift = sb("shift", [P, 2, TILES])
        zeros = sb("zeros", [H, NODES])
        eps = sb("eps", [P, 1])
        ident = sb("ident", [P, P])
        iota = sb("iota", [P, WIN])
        ones = sb("ones", [P, 1])
        one_row = sb("one_row", [1, P])
        bad = sb("bad", [P, 3])
        flag = sb("flag", [1, 1], i32)
        w = sb("w", [P, COLS])

        def part(name, rows=P):
            c, n = AT[name]
            return w[0:rows, c:c + n]

        wl0h, wl0e, wl1, wl2, wn1, wn2, wl0, wn0, bias1, bias2 = (
            part(n) for n in ("l0h", "l0e", "l1", "l2", "n1", "n2", "l0", "n0", "bias1", "bias2"))
        w1o_s, w2a_s, w2u_s, w2o_s, col = (part(n, H) for n in ("w1o", "w2a", "w2u", "w2o", "col"))
        bo_row = part("bo", 1)
        wno = sb("wno", [P, P])
        drop63 = sb("drop63", [H, H])
        lnw = sb("lnw", [H, 3, H])
        bo_all = sb("bo_all", [P, H])
        res = sb("res", [P, 2, 2 * HALF, H])
        slow_raw = sb("slow_raw", [SLOW, H])
        slow_rows = sb("slow_rows", [SLOW, 2, H])
        slow_idx = sb("slow_idx", [SLOW, 1], i32)
        slow_dst = sb("slow_dst", [1, SLOW], i32)
        slow_cen = sb("slow_cen", [SLOW, H])
        slow_diag = sb("slow_diag", [SLOW, SLOW])
        slow_msg = sb("slow_msg", [H, SLOW])

        def bank(name):
            return ctx.enter_context(nc.psum_tensor(name, [P, 512], f32))

        ps_ta, ps_tb, ps_l0, ps_l1, ps_l2, ps_agg = (bank(n) for n in ("ta", "tb", "l0", "l1", "l2", "agg"))
        ps_t2 = [bank("t2a"), bank("t2b")]
        AW = CPG * WIN
        ps_tab = [ps_ta, ps_tb, ps_l0, ps_l1, ps_l2, ps_t2[0], ps_t2[1]]

        s_ix = [sem("s_ix0"), sem("s_ix1")]
        s_nats, s_natd = sem("s_nats"), sem("s_natd")
        s_natm = sem("s_natm")
        s_w, s_base = sem("s_w"), sem("s_base")
        s_x = sem("s_x")
        s_const = sem("s_const")
        s_pool = sem("s_pool")
        s_natf = sem("s_natf")
        s_ln = sem("s_ln")
        s_bad = sem("s_bad")
        s_var, s_root = sem("s_var"), sem("s_root")
        s_nvar, s_nroot = sem("s_nvar"), sem("s_nroot")
        s_fvar, s_froot = sem("s_fvar"), sem("s_froot")
        s_tabp = sem("s_tabp")
        s_tabc = sem("s_tabc")
        s_hT = sem("s_hT")
        s_hTc = sem("s_hTc")
        s_wp = sem("s_wp")
        s_wc = sem("s_wc")
        s_flagp = sem("s_flagp")
        s_flag = sem("s_flag")
        s_free = [sem("s_free0"), sem("s_free1")]
        s_gath = [sem("s_gath0"), sem("s_gath1")]
        s_norm = sem("s_norm")
        s_attr = [sem("s_attr0"), sem("s_attr1")]
        s_tra, s_trb = sem("s_tra"), sem("s_trb")
        s_xa, s_xb = sem("s_xa"), sem("s_xb")
        s_l0, s_l1, s_l2 = sem("s_l0"), sem("s_l1"), sem("s_l2")
        s_h0, s_h1, s_h2 = sem("s_h0"), sem("s_h1"), sem("s_h2")
        s_t2 = sem("s_t2")
        s_rd = sem("s_rd")
        s_cen = sem("s_cen")
        s_oh = sem("s_oh")
        s_agg = sem("s_agg")
        s_add = sem("s_add")
        s_dve = sem("s_dve")
        s_st = sem("s_st")
        s_zero, s_zeroa = sem("s_zero"), sem("s_zeroa")
        s_fz, s_fload, s_fin, s_fg, s_frow, s_fT, s_fx, s_fU, s_fs, s_frd, s_fm, s_fc, s_fadd, s_fd = (
            sem("s_f_" + n) for n in ("zero", "load", "in", "gath", "row", "T", "x", "U", "chain", "rd", "m",
                                      "c", "add", "done"))
        s_fl, s_fh = [sem(f"s_fl{k}") for k in range(3)], [sem(f"s_fh{k}") for k in range(3)]
        s_sums = sem("s_sums")
        s_n0, s_n1, s_n2, s_nt, s_no = (sem(f"s_n{k}") for k in "012to")
        s_nh0, s_nh1, s_nh2 = (sem(f"s_nh{k}") for k in "012")
        s_nst, s_nres = sem("s_nst"), sem("s_nres")
        s_nscaled = sem("s_nscaled")
        s_xs = sem("s_xs")
        s_xhb = sem("s_xhb")
        s_out = [sem("s_out0"), sem("s_out1")]

        def attr_rows(e0, chunks, parts):
            return edge_attr[bass.ds(e0, (chunks - 1) * CHUNK + 2 * parts), :].rearrange(
                "(c p t) d -> p c (t d)", c=chunks, t=2)

        def node_rows(t, b0, b1):
            return t[b0 * NODES:b1 * NODES, :].rearrange("(b p t) d -> p b (t d)", p=P, t=HALF)

        def node_tail(t):
            return t[(NBLK - 1) * NODES:N, :].rearrange("(p t) d -> p (t d)", t=HALF)

        block = ctx.enter_context(nc.Block())

        def chunks_in(g):
            return TAILC if isinstance(g, int) and g == GROUPS - 1 else CPG

        def span(i):
            if not isinstance(i, int) or i >= T0:
                return NODE_T, ALLT
            return RAW_T, ALLT if i > 0 else OUT_T

        def mean_steps(link, parts, lo, hi):
            b = bn[0:parts, lo:hi, :]
            s = st[0:parts, :, lo:hi]
            link(nc.vector.tensor_tensor(s[:, 0, :], b[:, :, 1], b[:, :, 4], ALU.subtract))
            nc.vector.scalar_tensor_tensor(s[:, 2, :], s[:, 0, :], 0.25, s[:, 0, :], ALU.mult, ALU.mult)
            nc.vector.tensor_tensor(s[:, 3, :], b[:, :, 2], b[:, :, 5], ALU.add)
            link(nc.vector.scalar_tensor_tensor(s[:, 1, :], s[:, 0, :], -0.5, b[:, :, 1], ALU.mult, ALU.add))

        def var_step(parts, lo, hi):
            s = st[0:parts, :, lo:hi]
            return nc.vector.scalar_tensor_tensor(s[:, 4, :], s[:, 3, :], 1.0 / H, s[:, 2, :], ALU.mult, ALU.add)

        def root_step(parts, lo, hi):
            return nc.scalar.activation(st[0:parts, 5, lo:hi], st[0:parts, 4, lo:hi], ACT.Sqrt, bias=eps[0:parts, :])

        def rstd_steps(link, parts, lo, hi, k):
            s = st[0:parts, :, lo:hi]
            link(nc.vector.reciprocal(s[:, 5, :], s[:, 5, :]))
            link(nc.vector.tensor_tensor(s[:, 6, :], s[:, 5, :], s[:, 5, :], ALU.mult))
            link(nc.vector.scalar_tensor_tensor(s[:, 6, :], s[:, 4, :], EPS, s[:, 6, :], ALU.add, ALU.mult))
            link(nc.vector.tensor_scalar(s[:, 6, :], s[:, 6, :], -0.5, 1.5, ALU.mult, ALU.add))
            link(nc.vector.tensor_tensor(rstd[0:parts, k, lo:hi], s[:, 5, :], s[:, 6, :], ALU.mult))

        @block.sync
        def _(sp):
            for g in range(2):
                sp.dma_start(idx[:, g, :].rearrange("p (c t) -> p c t", t=2),
                             src[g * GROUP:(g + 1) * GROUP].rearrange("(c p t) -> p c t", p=P, t=2)).then_inc(s_ix[g], 16)
            sp.wait_ge(s_natm, 2)
            full = E // (P * CHUNK)
            rest = (E - full * P * CHUNK) // CHUNK
            left = E - (full * P + rest) * CHUNK
            for k, (a, landed) in enumerate(((src, s_nats), (dst, s_natd))):
                if full:
                    sp.dma_start(nat[:, k, 0:full, :],
                                 a[0:full * P * CHUNK].rearrange("(b p e) -> p b e", p=P, e=CHUNK)).then_inc(landed, 16)
                if rest:
                    sp.dma_start(nat[0:rest, k, full, :],
                                 a[full * P * CHUNK:(full * P + rest) * CHUNK].rearrange("(p e) -> p e", e=CHUNK)
                                 ).then_inc(landed, 16)
                if left:
                    sp.dma_start(nat[rest:rest + 1, k, full, 0:left],
                                 a[E - left:E].rearrange("(p e) -> p e", p=1)).then_inc(landed, 16)
            for g in range(2):
                sp.dma_start(rows[:, g, 1, :, :].rearrange("p (c t) d -> p c (t d)", t=2),
                             attr_rows(g * GROUP, CPG, P)).then_inc(s_attr[g], 16)
            sp.wait_ge(s_zero, 1)
            with nc.allow_non_contiguous_dma("one value of each chunk"):
                sp.dma_start(base_row[0:1, 0:REALC],
                             dst.rearrange("(o e) -> o e", o=1)[:, 0:(REALC - 1) * CHUNK + 1:CHUNK]).then_inc(s_base, 16)

            def load_attr(g, k):
                sp.wait_ge(s_trb, g - 1)
                sp.dma_start(rows[:, k, 1, :, :].rearrange("p (c t) d -> p c (t d)", t=2),
                             attr_rows(g * GROUP, CPG, P)).then_inc(s_attr[k], 16)

            def load_x(pieces):
                for b0, b1 in pieces:
                    sp.dma_start(xn[:, b0 * HALF:b1 * HALF, :].rearrange("p (b t) d -> p b (t d)", t=HALF),
                                 node_rows(x, b0, b1)).then_inc(s_x, 16)

            sp.wait_ge(s_norm, 1)
            load_x(XPIECES[0:1])
            load_attr(2, 0)
            load_x(XPIECES[1:3])
            load_attr(3, 1)
            load_x(XPIECES[3:])
            sp.wait_ge(s_zero, 2)
            sp.dma_start(xn[0:LASTP, (NBLK - 1) * HALF:NBLK * HALF, :].rearrange("p t d -> p (t d)"),
                         node_tail(x)).then_inc(s_x, 16)
            with sp.Fori(4, GROUPS - 2, 2) as g:
                load_attr(g, 0)
                load_attr(g + 1, 1)
            load_attr(GROUPS - 2, 0)
            g = GROUPS - 1
            sp.wait_ge(s_trb, g - 1)
            for c in range(TAILC):
                n = min(CHUNK, E - g * GROUP - c * CHUNK) // 2
                sp.dma_start(rows[0:n, 1, 1, 2 * c:2 * c + 2, :].rearrange("p t d -> p (t d)"),
                             attr_rows(g * GROUP + c * CHUNK, 1, n).rearrange("p c d -> p (c d)")).then_inc(s_attr[1], 16)

            sp.wait_ge(s_flag, 1)
            f = sp.value_load(flag[0:1, 0:1], min_val=0, max_val=P)
            with sp.If(f > 0):
                with sp.Fori(1, E // SLOW + 1) as v:
                    sp.wait_ge(s_fd, v)
                    e0 = v * SLOW - SLOW
                    sp.dma_start(slow_idx[:, :], src[bass.ds(e0, SLOW)].rearrange("(p o) -> p o", o=1)).then_inc(s_fload, 16)
                    sp.dma_start(slow_dst[:, :], dst[bass.ds(e0, SLOW)].rearrange("(o e) -> o e", o=1)).then_inc(s_fload, 16)
                    sp.dma_start(slow_rows[:, 1, :], edge_attr[bass.ds(e0, SLOW), :]).then_inc(s_fload, 16)
                    sp.wait_ge(s_fload, v * 48)
                    sp.sem_inc(s_fin, 1)

            for q in range(PAIRS):
                sp.wait_ge(s_nres, q + 1)
                b0, b1 = 2 * q, min(2 * q + 2, NBLK)
                fb = b1 - 1 if b1 == NBLK else b1
                if fb > b0:
                    sp.dma_start(node_rows(out, b0, fb),
                                 res[:, q % 2, 0:(fb - b0) * HALF, :].rearrange("p (b t) d -> p b (t d)", t=HALF)
                                 ).then_inc(s_out[q % 2], 16)
                if b1 == NBLK:
                    sp.dma_start(node_tail(out), res[0:LASTP, q % 2, (fb - b0) * HALF:(fb - b0 + 1) * HALF, :]
                                 .rearrange("p t d -> p (t d)")).then_inc(s_out[q % 2], 16)
            for k in range(2):
                sp.wait_ge(s_out[k], OUTS[k])

        @block.gpsimd
        def _(pool):
            pool.memset(nat[:, 0, CBLK - 1, :], 0).then_inc(s_natm, 1)
            pool.memset(nat[:, 1, CBLK - 1, :], int(PAD)).then_inc(s_natm, 1)
            pool.memset(ident[:, :], 0.0)
            pool.memset(drop63[:, :], 0.0)
            pool.memset(ones[:, :], 1.0)
            pool.memset(eps[:, :], EPS)
            pool.memset(one_row[:, :], 1.0)
            pool.memset(lnw[:, 2, :], -1.0 / H)
            pool.iota(iota[:, :], pattern=[[1, WIN]], base=0, channel_multiplier=0,
                      allow_small_or_imprecise_dtypes=True).then_inc(s_pool, 1)
            pool.wait_ge(s_pool, 1)
            pool.affine_select(out=ident[:, :], in_=ident[:, :], compare_op=ALU.not_equal, fill=1.0,
                               base=0, pattern=[[-1, P]], channel_multiplier=1)
            pool.affine_select(out=drop63[:, :], in_=drop63[:, :], compare_op=ALU.not_equal, fill=-1.0,
                               base=1 - H, pattern=[[0, H]], channel_multiplier=1).then_inc(s_pool, 1)
            pool.wait_ge(s_pool, 2)
            pool.affine_select(out=drop63[:, :], in_=drop63[:, :], compare_op=ALU.not_equal, fill=1.0,
                               base=0, pattern=[[-1, H]], channel_multiplier=1)
            pool.tensor_tensor(lnw[:, 2, :], lnw[:, 2, :], ident[0:H, 0:H], ALU.add).then_inc(s_const, 1)

            def gather(k, tiles):
                for j in range(tiles):
                    pool.indirect_dma_start(
                        out=raw[:, k, j, :], out_offset=None, in_=x,
                        in_offset=bass.IndirectOffsetOnAxis(ap=idx[:, k, j:j + 1], axis=0)).then_inc(s_gath[k], 16)

            for k in range(2):
                pool.wait_ge(s_ix[k], 16)
                gather(k, TILES)
            with pool.Fori(1, GROUPS // 2 - 1) as v:
                for k in range(2):
                    pool.wait_ge(s_ix[k], 16)
                    pool.wait_ge(s_free[k], v)
                    gather(k, TILES)
            pool.wait_ge(s_flag, 1)
            f = pool.value_load(flag[0:1, 0:1], min_val=0, max_val=P)
            pool.wait_ge(s_free[0], GROUPS // 2 - 1)
            gather(0, TILES)
            pool.wait_ge(s_free[1], GROUPS // 2 - 1)
            gather(1, 2 * TAILC)

            with pool.If(f > 0):
                with pool.Fori(1, E // SLOW + 1) as v:
                    pool.wait_ge(s_ix[0], 16)
                    pool.wait_ge(s_fin, v)
                    pool.indirect_dma_start(
                        out=slow_raw[:, :], out_offset=None, in_=x,
                        in_offset=bass.IndirectOffsetOnAxis(ap=slow_idx[:, 0:1], axis=0)).then_inc(s_fg, 16)

            pool.wait_ge(s_xs, PARTS)
            for q in range(PAIRS):
                xq = xn[:, q * TILES:(q + 1) * TILES, :]
                pool.tensor_tensor(xq, xq, bo_all[:, :].unsqueeze(1).to_broadcast([P, TILES, H]), ALU.add).then_inc(s_xhb, 1)
            for q in range(PAIRS):
                pool.wait_ge(s_xhb, q + 1)
                pool.wait_ge(s_nscaled, q + 1)
                r = res[:, q % 2, :, :]
                pool.tensor_tensor(r, r, xn[:, q * TILES:(q + 1) * TILES, :], ALU.add).then_inc(s_nres, 1)

        @block.scalar
        def _(act):
            act.dma_start(w[:, :], packed).then_inc(s_w, 16)
            act.wait_ge(s_zero, 1)
            for c0 in range(ZSPLIT, AGGW, NODES):
                n = min(NODES, AGGW - c0)
                last = act.activation(node_in[0:H, c0:c0 + n], zeros[:, 0:n], ACT.Copy)
            last.then_inc(s_zeroa, 1)
            for n in range(TABS):
                k, q = divmod(n, TABK)
                act.wait_ge(s_tabp, n + 1)
                tab = (src_tab, dst_tab)[k]
                b0, b1 = 2 * q, min(2 * q + 2, CBLK)
                act.activation(tab[:, b0 * P:b1 * P, :].rearrange("p (b c) t -> p b t c", c=P),
                               ps_tab[n % 7][:, 0:(b1 - b0) * 2 * P].rearrange("p (b t c) -> p b t c", t=2, c=P),
                               ACT.Copy).then_inc(s_tabc, 1)

            def edge_iter(i, k, opens, mid, late, nodes, after):
                if mid:
                    act.wait_ge(s_l2, i)
                    c = chunks_in(i - 1) * P
                    act.activation(h2[:, 0:c], ps_l2[:, 0:c], ACT.Relu, bias=bias1[:, 2:3]).then_inc(s_h2, 1)
                n = chunks_in(i) * P
                if opens:
                    act.wait_ge(s_tra, i + 1)
                    act.activation(xT[:, 0:n], ps_ta[:, 0:n], ACT.Copy).then_inc(s_xa, 1)
                if late:
                    act.wait_ge(s_rd, i - 1)
                    for q in range(2 * chunks_in(i - 2)):
                        last = act.activation(cen[:, k, q, 0:H - 1], ps_t2[k][:, q * H:(q + 1) * H - 1], ACT.Identity,
                                              scale=rstd[:, 1 - k, OUT_T + q:OUT_T + q + 1], bias=shift[:, 1 - k, q:q + 1])
                    last.then_inc(s_cen, 1)
                if opens:
                    act.wait_ge(s_l0, i + 1)
                    act.activation(h0[:, 0:n], ps_l0[:, 0:n], ACT.Relu, bias=bias1[:, 0:1]).then_inc(s_h0, 1)
                if opens or mid:
                    act.wait_ge(s_var, i + 2)
                    root_step(P, *span(i)).then_inc(s_root, 1)
                if after:
                    act.wait_ge(s_trb, i + 2)
                    c = chunks_in(i + 1) * P
                    act.activation(xT[:, GROUP // 2:GROUP // 2 + c], ps_tb[:, 0:c], ACT.Copy).then_inc(s_xb, 1)
                if nodes is not None:
                    act.wait_ge(s_hT, i - T0)
                    act.activation(node_in[H:P, bass.ds(nodes * NODES, NODES)]
                                   .rearrange("d (p t) -> d t p", t=HALF)[:, (1 - k) * NPT:(2 - k) * NPT, :],
                                   ps_agg[H:P, 0:NPT * P].rearrange("d (t p) -> d t p", p=P), ACT.Copy).then_inc(s_hTc, 1)
                if opens:
                    act.wait_ge(s_l1, i + 1)
                    act.activation(h1[:, 0:n], ps_l1[:, 0:n], ACT.Relu, bias=bias1[:, 1:2]).then_inc(s_h1, 1)

            act.wait_ge(s_w, 16)
            act.wait_ge(s_var, 1)
            root_step(P, RAW_T, OUT_T).then_inc(s_root, 1)
            act.wait_ge(s_trb, 1)
            act.activation(xT[:, GROUP // 2:GROUP], ps_tb[:, :], ACT.Copy).then_inc(s_xb, 1)
            edge_iter(0, 0, True, False, 0, None, True)
            edge_iter(1, 1, True, True, 0, None, True)
            for i in (2, 3, 4):
                edge_iter(i, i % 2, True, True, 1, None, True)
            with act.Fori(2, PARTS // 2 + 2) as n:
                edge_iter(n * 2 + 1, 1, True, True, 1, n - 2, True)
                edge_iter(n * 2 + 2, 0, True, True, 1, n - 2, True)
            act.wait_ge(s_flagp, 1)
            act.activation(flag[0:1, 0:1], ps_agg[H:H + 1, 0:1], ACT.Copy).then_inc(s_flag, 1)
            with act.Fori(PARTS // 2 + 2, GROUPS // 2 - 2) as n:
                edge_iter(n * 2 + 1, 1, True, True, 1, None, True)
                edge_iter(n * 2 + 2, 0, True, True, 1, None, True)
            act.wait_ge(s_flag, 1)
            f = act.value_load(flag[0:1, 0:1], min_val=0, max_val=P)
            edge_iter(GROUPS - 3, 1, True, True, 1, None, True)
            edge_iter(GROUPS - 2, 0, True, True, 1, None, True)
            edge_iter(GROUPS - 1, 1, True, True, 1, None, False)
            edge_iter(GROUPS, 0, False, True, 1, None, False)
            edge_iter(GROUPS + 1, 1, False, False, 1, None, False)

            with act.If(f > 0):
                with act.Fori(1, E // SLOW + 1) as v:
                    act.wait_ge(s_fvar, v * 2 - 1)
                    root_step(SLOW, 0, 1).then_inc(s_froot, 1)
                    act.wait_ge(s_fT, v)
                    act.activation(xT[:, 0:SLOW], ps_ta[:, 0:SLOW], ACT.Copy).then_inc(s_fx, 1)
                    for k, (ps, h) in enumerate(((ps_l0, h0), (ps_l1, h1), (ps_l2, h2))):
                        act.wait_ge(s_fl[k], v)
                        act.activation(h[0:H, 0:SLOW], ps[0:H, 0:SLOW], ACT.Relu, bias=bias1[0:H, k:k + 1]).then_inc(s_fh[k], 1)
                    act.wait_ge(s_fvar, v * 2)
                    root_step(SLOW, 0, 1).then_inc(s_froot, 1)

            act.wait_ge(s_wc, WC)
            for q in range(PAIRS + 1):
                if q < PAIRS:
                    act.wait_ge(s_n0, q + 1)
                    if q:
                        act.wait_ge(s_n1, q)
                    act.activation(h0[:, :], ps_l0[:, :], ACT.Relu, bias=bias2[:, 0:1]).then_inc(s_nh0, 1)
                if q > 1:
                    act.wait_ge(s_nvar, q - 1)
                    root_step(P, 0, TILES).then_inc(s_nroot, 1)
                if q:
                    act.wait_ge(s_n2, q)
                    if q > 1:
                        act.wait_ge(s_no, q - 1)
                    act.activation(h2[:, :], ps_l2[:, :], ACT.Relu, bias=bias2[:, 2:3]).then_inc(s_nh2, 1)
                if q < PAIRS:
                    act.wait_ge(s_n1, q + 1)
                    if q:
                        act.wait_ge(s_n2, q)
                    act.activation(h1[:, :], ps_l1[:, :], ACT.Relu, bias=bias2[:, 1:2]).then_inc(s_nh1, 1)

            act.wait_ge(s_nvar, PAIRS)
            root_step(P, 0, TILES).then_inc(s_nroot, 1)

        @block.vector
        def _(dve):
            dve.memset(zeros[:, :], 0.0)
            dve.memset(base_row[:, :], 0).then_inc(s_zero, 1)
            dve.memset(xn[:, (NBLK - 1) * HALF:NBE * HALF, :], 0.0).then_inc(s_zero, 1)
            dve.memset(node_in[0:H, 0:ZSPLIT], 0.0)
            dve.memset(wno[:, :], 0.0)
            dve.memset(cen[:, :, :, H - 1], 1.0).then_inc(s_zero, 1)
            chain = [0]

            def link(ins):
                chain[0] += 1
                ins.then_inc(s_dve, 1)
                dve.wait_ge(s_dve, chain[0])

            dve.wait_ge(s_nats, 16 * NATS)
            nc.vector.tensor_copy(natf[:, 0, :, :], nat[:, 0, :, :]).then_inc(s_natf, 1)
            dve.wait_ge(s_natd, 16 * NATS)
            link(nc.vector.tensor_copy(natf[:, 1, :, :], nat[:, 1, :, :]))
            link(nc.vector.tensor_scalar(base_f[:, :], natf[:, 1, :, 0], 0.0, None, ALU.max))
            nc.vector.tensor_tensor(natf[:, 1, :, :], natf[:, 1, :, :],
                                    base_f[:, :].unsqueeze(2).to_broadcast([P, CBLK, CHUNK]),
                                    ALU.subtract).then_inc(s_natf, 1)

            dve.wait_ge(s_w, 16)
            dve.wait_ge(s_const, 1)
            link(nc.vector.tensor_scalar(lnw[:, 0, :], drop63[:, :], col[:, 0:1], None, ALU.mult))
            nc.vector.tensor_copy(lnw[:, 0, H - 1:H], col[:, 1:2]).then_inc(s_wc, 1)
            dve.wait_ge(s_wp, 1)
            link(nc.vector.tensor_copy(lnw[:, 1, :], ps_agg[0:H, 0:H]))
            nc.vector.tensor_tensor(lnw[:, 1, H - 1:H], lnw[:, 1, H - 1:H], col[:, 2:3], ALU.add).then_inc(s_wc, 1)
            dve.wait_ge(s_wp, 2)
            nc.vector.tensor_copy(wn0[0:H, :], ps_agg[0:H, 64:64 + H])
            nc.vector.tensor_tensor(bias2[0:H, 0:1], bias2[0:H, 0:1], ps_agg[0:H, 128:129], ALU.add)
            nc.vector.tensor_tensor(bias2[H:P, 0:1], bias2[H:P, 0:1], ps_agg[H:P, 128:129], ALU.add)
            link(nc.vector.tensor_tensor(bo_row[:, :], bo_row[:, :], ps_agg[0:1, 256:256 + H], ALU.add))
            nc.vector.tensor_scalar(w2o_s[:, :], w2o_s[:, :], col[:, 4:5], None, ALU.mult).then_inc(s_wc, 1)
            dve.wait_ge(s_wp, 3)
            nc.vector.tensor_copy(wno[0:H, 0:H], ps_agg[0:H, 320:320 + H])
            nc.vector.tensor_copy(wno[H:P, H:P], ps_agg[H:P, 320:320 + H])
            nc.vector.tensor_copy(bo_all[:, :], ps_agg[:, 384:384 + H]).then_inc(s_wc, 1)

            base_regs = [dve.alloc_register(f"window_base{c}") for c in range(CPG)]

            def edge_iter(i, k, gathered, stage, mid, agg, nodes):
                j = 1 - k
                lo, hi = span(i)
                raws, outs = 2 * chunks_in(i + 1), 2 * chunks_in(i - 1)
                if agg:
                    a = i - 2
                    dve.reg_load(base_regs, base_row[0:1, bass.ds(a * CPG, CPG)])
                    bases = [dve.snap(reg, min_val=0, max_val=N - 1) for reg in base_regs]

                def add_window(c):
                    if agg and c < chunks_in(i - 2):
                        if agg > 1 or c:
                            dve.wait_ge(s_add, a * CPG + c)
                        win = node_in[0:H, bass.ds(bases[c], WIN)]
                        nc.vector.tensor_tensor(win, win, ps_agg[0:H, k * AW + c * WIN:k * AW + (c + 1) * WIN],
                                                ALU.add).then_inc(s_add, 1)

                base = i * 8 + 8
                if gathered is not None:
                    dve.wait_ge(s_gath[j], gathered)
                    for q in range(raws):
                        last = nc.vector.bn_stats(bn[:, RAW_T + q, :], raw[:, j, q, :])
                if nodes is not None:
                    xb = xn[:, bass.ds(nodes * NPT, NPT), :]
                    for q in range(NPT):
                        last = nc.vector.bn_stats(bn[:, NODE_T + q, :], xb[:, q, :])
                if mid:
                    dve.wait_ge(s_t2, i)
                    ps = ps_t2[j][:, :].rearrange("p (q d) -> p q d", d=H)
                    for q in range(outs):
                        last = nc.vector.bn_stats(bn[:, OUT_T + q, :], ps[:, q, :])
                stats = gathered is not None or mid
                b, s = bn[:, lo:hi, :], st[:, :, lo:hi]
                if stats:
                    last.then_inc(s_st, 1)
                if mid:
                    nc.vector.tensor_tensor(
                        onehot[:, j, 0:outs, :], iota[:, :].unsqueeze(1).to_broadcast([P, outs, WIN]),
                        dst_tab[:, bass.ds(i * CPG - CPG, chunks_in(i - 1)), :].rearrange("p c t -> p (c t)").unsqueeze(2)
                        .to_broadcast([P, outs, WIN]), ALU.is_equal).then_inc(s_oh, 1)
                if stats:
                    dve.wait_ge(s_st, base + 1)
                    nc.vector.tensor_tensor(s[:, 0, :], b[:, :, 1], b[:, :, 4], ALU.subtract).then_inc(s_st, 1)
                    nc.vector.tensor_tensor(s[:, 3, :], b[:, :, 2], b[:, :, 5], ALU.add)
                    dve.wait_ge(s_st, base + 2)
                    nc.vector.scalar_tensor_tensor(s[:, 1, :], s[:, 0, :], -0.5, b[:, :, 1], ALU.mult, ALU.add)
                    nc.vector.scalar_tensor_tensor(s[:, 2, :], s[:, 0, :], 0.25, s[:, 0, :], ALU.mult, ALU.mult).then_inc(s_st, 1)
                if stage:
                    nc.vector.tensor_copy(idx[:, j, :], src_tab[:, bass.ds(i * CPG + 3 * CPG, CPG), :]
                                          .rearrange("p c t -> p (c t)"))
                if stats:
                    dve.wait_ge(s_st, base + 3)
                    var_step(P, lo, hi).then_inc(s_var, 1)
                if gathered is not None:
                    nc.vector.tensor_tensor(rows[:, j, 0, 0:raws, :], raw[:, j, 0:raws, :],
                                            st[:, 1, RAW_T:RAW_T + raws].unsqueeze(2).to_broadcast([P, raws, H]),
                                            ALU.subtract).then_inc(s_free[j], 1)
                if nodes is not None:
                    nc.vector.tensor_tensor(hs[:, k, :, :], xb, st[:, 1, NODE_T:RAW_T].unsqueeze(2)
                                            .to_broadcast([P, NPT, H]), ALU.subtract)
                if agg:
                    dve.wait_ge(s_agg, i - 1)
                if stats:
                    dve.wait_ge(s_root, i + 2)
                    nc.vector.reciprocal(s[:, 5, :], s[:, 5, :]).then_inc(s_st, 1)
                    add_window(0)
                    dve.wait_ge(s_st, base + 4)
                    nc.vector.tensor_tensor(s[:, 6, :], s[:, 5, :], s[:, 5, :], ALU.mult).then_inc(s_st, 1)
                    add_window(1)
                    dve.wait_ge(s_st, base + 5)
                    nc.vector.scalar_tensor_tensor(s[:, 6, :], s[:, 4, :], EPS, s[:, 6, :], ALU.add, ALU.mult).then_inc(s_st, 1)
                    add_window(2)
                    dve.wait_ge(s_st, base + 6)
                    nc.vector.tensor_scalar(s[:, 6, :], s[:, 6, :], -0.5, 1.5, ALU.mult, ALU.add).then_inc(s_st, 1)
                    add_window(3)
                    dve.wait_ge(s_st, base + 7)
                    nc.vector.tensor_tensor(rstd[:, k, lo:hi], s[:, 5, :], s[:, 6, :], ALU.mult).then_inc(s_st, 1)
                    dve.wait_ge(s_st, base + 8)
                else:
                    for c in range(CPG):
                        add_window(c)
                if mid:
                    nc.vector.scalar_tensor_tensor(shift[:, k, :], st[:, 1, OUT_T:ALLT], -1.0, rstd[:, k, OUT_T:ALLT],
                                                   ALU.mult, ALU.mult).then_inc(s_rd, 1)
                if gathered is not None:
                    nc.vector.scalar_tensor_tensor(rows[:, j, 0, 0:raws, :], rows[:, j, 0, 0:raws, :], 0.0,
                                                   rstd[:, k, RAW_T:RAW_T + raws].unsqueeze(2).to_broadcast([P, raws, H]),
                                                   ALU.max, ALU.mult).then_inc(s_norm, 1)
                if nodes is not None:
                    nc.vector.scalar_tensor_tensor(hs[:, k, :, :], hs[:, k, :, :], 0.0,
                                                   rstd[:, k, NODE_T:RAW_T].unsqueeze(2).to_broadcast([P, NPT, H]),
                                                   ALU.max, ALU.mult).then_inc(s_ln, 1)
                    dve.wait_ge(s_ln, i + 1 - T0)
                    nc.vector.tensor_tensor(xb, xb, hs[:, k, :, :], ALU.add).then_inc(s_xs, 1)

            GV = 16 * TILES
            dve.wait_ge(s_tabc, TABK)
            edge_iter(-1, 1, GV, True, False, 0, None)
            edge_iter(0, 0, GV, True, False, 0, None)

            dve.wait_ge(s_natf, 2)
            d = natf[:, 1, :, :].rearrange("p b e -> p (b e)")
            real = nat[:, 1, :, :].rearrange("p b e -> p (b e)").bitcast(f32)
            link(nc.vector.tensor_reduce(bad[:, 0:1], d, AX.X, ALU.max))
            edge_iter(1, 1, 2 * GV, True, True, 0, None)
            link(nc.vector.scalar_tensor_tensor(real, d, PAD / 2, d, ALU.is_gt, ALU.mult))
            dve.wait_ge(s_zero, 3)
            dve.wait_ge(s_zeroa, 1)
            dve.wait_ge(s_base, 16)
            edge_iter(2, 0, 2 * GV, True, True, 1, None)
            link(nc.vector.tensor_reduce(bad[:, 1:2], real, AX.X, ALU.min))
            link(nc.vector.tensor_scalar(bad[:, 2:3], bad[:, 0:1], float(WIN - 1), None, ALU.is_gt))
            nc.vector.scalar_tensor_tensor(bad[:, 2:3], bad[:, 1:2], 0.0, bad[:, 2:3],
                                           ALU.is_lt, ALU.max).then_inc(s_bad, 1)
            edge_iter(3, 1, 3 * GV, True, True, 2, None)
            dve.wait_ge(s_x, 16 * (len(XPIECES) + 1))
            with dve.Fori(2, PARTS // 2 + 2) as n:
                edge_iter(n * 2, 0, n * GV + GV, True, True, 2, n * 2 - 4)
                edge_iter(n * 2 + 1, 1, n * GV + 2 * GV, True, True, 2, n * 2 - 3)
            with dve.Fori(PARTS // 2 + 2, GROUPS // 2 - 2) as n:
                edge_iter(n * 2, 0, n * GV + GV, True, True, 2, None)
                edge_iter(n * 2 + 1, 1, n * GV + 2 * GV, True, True, 2, None)
            n = GROUPS // 2
            dve.wait_ge(s_flag, 1)
            f = dve.value_load(flag[0:1, 0:1], min_val=0, max_val=P)
            edge_iter(GROUPS - 4, 0, (n - 1) * GV, True, True, 2, None)
            edge_iter(GROUPS - 3, 1, n * GV, False, True, 2, None)
            edge_iter(GROUPS - 2, 0, (n - 1) * GV + 32 * TAILC, False, True, 2, None)
            edge_iter(GROUPS - 1, 1, None, False, True, 2, None)
            edge_iter(GROUPS, 0, None, False, True, 2, None)
            edge_iter(GROUPS + 1, 1, None, False, False, 2, None)

            dve.wait_ge(s_add, REALC)
            with dve.If(f > 0):
                dve.memset(node_in[0:H, :], 0.0).then_inc(s_fz, 1)
                dve.wait_ge(s_fz, 1)
                dve.sem_inc(s_fd, 1)
                dve.sem_inc(s_fadd, 1)
                with dve.Fori(1, E // SLOW + 1) as v:
                    step = [0]

                    def link(ins):
                        step[0] += 1
                        ins.then_inc(s_fs, 1)
                        dve.wait_ge(s_fs, v * 16 - 16 + step[0])

                    dve.wait_ge(s_fg, v * 16)
                    link(nc.vector.bn_stats(bn[0:SLOW, 0, :], slow_raw[:, :]))
                    mean_steps(link, SLOW, 0, 1)
                    nc.vector.tensor_scalar(slow_rows[:, 0, :], slow_raw[:, :], st[0:SLOW, 1, 0:1], None, ALU.subtract)
                    var_step(SLOW, 0, 1).then_inc(s_fvar, 1)
                    dve.wait_ge(s_froot, v * 2 - 1)
                    rstd_steps(link, SLOW, 0, 1, 0)
                    nc.vector.tensor_scalar(slow_rows[:, 0, :], slow_rows[:, 0, :], 0.0, rstd[0:SLOW, 0, 0:1],
                                            ALU.max, ALU.mult).then_inc(s_frow, 1)
                    dve.wait_ge(s_fU, v)
                    link(nc.vector.bn_stats(bn[0:SLOW, 0, :], ps_t2[0][0:SLOW, 0:H]))
                    mean_steps(link, SLOW, 0, 1)
                    nc.vector.tensor_scalar(slow_cen[:, :], ps_t2[0][0:SLOW, 0:H], st[0:SLOW, 1, 0:1], None, ALU.subtract)
                    var_step(SLOW, 0, 1).then_inc(s_fvar, 1)
                    dve.wait_ge(s_froot, v * 2)
                    rstd_steps(link, SLOW, 0, 1, 0)
                    nc.vector.scalar_tensor_tensor(slow_cen[:, H - 1:H], st[0:SLOW, 4, 0:1], EPS,
                                                   rstd[0:SLOW, 0, 0:1], ALU.add, ALU.mult)
                    nc.vector.tensor_scalar(slow_diag[:, :], ident[0:SLOW, 0:SLOW], rstd[0:SLOW, 0, 0:1],
                                            None, ALU.mult).then_inc(s_frd, 1)
                    dve.wait_ge(s_fm, v)
                    nc.vector.tensor_copy(slow_msg[:, :], ps_tb[0:H, 0:SLOW]).then_inc(s_fc, 1)
                    dve.wait_ge(s_fz, 1)
                    dve.wait_ge(s_fc, v)
                    with dve.Fori(0, SLOW) as e:
                        node = dve.value_load(slow_dst[0:1, bass.ds(e, 1)], min_val=0, max_val=N - 1)
                        dve.wait_ge(s_fadd, v * SLOW + e - (SLOW - 1))
                        c = node_in[0:H, bass.ds(node, 1)]
                        nc.vector.tensor_tensor(c, c, slow_msg[:, bass.ds(e, 1)], ALU.add).then_inc(s_fadd, 1)
                    dve.wait_ge(s_fadd, v * SLOW + 1)
                    dve.sem_inc(s_fd, 1)
            dve.sem_inc(s_sums, 1)

            for q in range(PAIRS):
                step = [0]

                def link(ins):
                    step[0] += 1
                    ins.then_inc(s_nst, 1)
                    dve.wait_ge(s_nst, q * 8 + step[0])

                dve.wait_ge(s_nt, q + 1)
                ps = ps_t2[0][:, :].rearrange("p (k h d) -> p (k h) d", h=2, d=H)
                for t in range(TILES):
                    last = nc.vector.bn_stats(bn[:, t, :], ps[:, t, :])
                link(last)
                mean_steps(link, P, 0, TILES)
                var_step(P, 0, TILES).then_inc(s_nvar, 1)
                dve.wait_ge(s_nroot, q + 1)
                rstd_steps(link, P, 0, TILES, q % 2)
                dve.wait_ge(s_no, q + 1)
                if q >= 2:
                    dve.wait_ge(s_out[q % 2], 16 * (q // 2))
                po = (ps_ta, ps_tb)[q % 2][:, :].rearrange("p (t h d) -> p t h d", h=2, d=H)
                nc.vector.tensor_tensor(res[:, q % 2, :, :].rearrange("p (h t) d -> p t h d", h=2), po,
                                        rstd[:, q % 2, 0:TILES].rearrange("p (t h) -> p t h", h=2).unsqueeze(3)
                                        .to_broadcast([P, HALF, 2, H]), ALU.mult).then_inc(s_nscaled, 1)

        @block.tensor
        def _(pe):
            pe.wait_ge(s_const, 1)
            for n in range(TABS):
                k, q = divmod(n, TABK)
                if q == 0:
                    pe.wait_ge(s_natf, k + 1)
                if n >= 7:
                    pe.wait_ge(s_tabc, n - 6)
                for b in range(2 * q, min(2 * q + 2, CBLK)):
                    for t in range(2):
                        o = (b - 2 * q) * 2 * P + t * P
                        last = pe.transpose(ps_tab[n % 7][:, o:o + P],
                                            natf[:, k, b, :].rearrange("c (p t) -> c t p", t=2)[:, t, :], ident[:, :])
                last.then_inc(s_tabp, 1)
            pe.wait_ge(s_w, 16)
            pe.wait_ge(s_wc, 1)
            pe.matmul(ps_agg[0:H, 0:H], w1o_s[:, :], lnw[:, 0, :], start=True, stop=True).then_inc(s_wp, 1)
            pe.wait_ge(s_wc, 2)
            pe.matmul(ps_agg[0:H, 64:64 + H], lnw[:, 1, :], w2a_s[:, :], start=True, stop=True)
            pe.matmul(ps_agg[0:H, 128:129], w2u_s[:, :], col[:, 3:4], start=True, stop=True)
            pe.matmul(ps_agg[H:P, 128:129], w2u_s[:, :], col[:, 3:4], start=True, stop=True)
            pe.matmul(ps_agg[0:1, 256:256 + H], col[:, 5:6], w2o_s[:, :], start=True, stop=True).then_inc(s_wp, 1)
            pe.wait_ge(s_wc, 3)
            pe.matmul(ps_agg[0:H, 320:320 + H], lnw[:, 2, :], w2o_s[:, :], start=True, stop=True)
            pe.matmul(ps_agg[H:P, 320:320 + H], lnw[:, 2, :], w2o_s[:, :], start=True, stop=True)
            pe.matmul(ps_agg[:, 384:384 + H], one_row[:, :], bo_row[:, :], start=True, stop=True).then_inc(s_wp, 1)
            pe.wait_ge(s_wc, WC)
            pe.wait_ge(s_tabc, TABS)

            def attrs_turned(g, k, attrs):
                pe.wait_ge(s_attr[k], attrs)
                for c in range(chunks_in(g)):
                    last = pe.transpose(ps_tb[:, c * P:(c + 1) * P],
                                        rows[:, k, 1, 2 * c:2 * c + 2, :].rearrange("p t d -> p (t d)"), ident[:, :])
                last.then_inc(s_trb, 1)

            def edge_iter(i, k, opens, mid, agg, attrs, nodes):
                if mid:
                    pe.wait_ge(s_h1, i)
                    m = chunks_in(i - 1) * P
                    pe.matmul(ps_l2[:, 0:m], wl2[:, :], h1[:, 0:m], start=True, stop=True).then_inc(s_l2, 1)
                n = chunks_in(i) * P
                if opens:
                    pe.wait_ge(s_norm, i + 1)
                    for c in range(chunks_in(i)):
                        last = pe.transpose(ps_ta[:, c * P:(c + 1) * P],
                                            rows[:, k, 0, 2 * c:2 * c + 2, :].rearrange("p t d -> p (t d)"), ident[:, :])
                    last.then_inc(s_tra, 1)
                if mid:
                    pe.wait_ge(s_h2, i)
                    for t in range(chunks_in(i - 1)):
                        last = pe.transpose(ps_t2[1 - k][:, t * P:(t + 1) * P], h2[:, t * P:(t + 1) * P], ident[:, :])
                    last.then_inc(s_t2, 1)
                if opens:
                    pe.wait_ge(s_xb, i + 1)
                    pe.matmul(ps_l0[:, 0:n], wl0e[:, :], xT[:, GROUP // 2:GROUP // 2 + n], start=True, stop=False)
                    pe.wait_ge(s_xa, i + 1)
                    pe.matmul(ps_l0[:, 0:n], wl0h[:, :], xT[:, 0:n], start=False, stop=True).then_inc(s_l0, 1)
                if attrs is not None:
                    attrs_turned(i + 1, 1 - k, attrs)
                if agg:
                    pe.wait_ge(s_cen, i - 1)
                    pe.wait_ge(s_oh, i - 1)
                    for c in range(chunks_in(i - 2)):
                        for t in range(2):
                            o = k * AW + c * WIN
                            last = pe.matmul(ps_agg[0:H, o:o + WIN], cen[:, k, 2 * c + t, :],
                                             onehot[:, k, 2 * c + t, :], start=(t == 0), stop=(t == 1))
                    last.then_inc(s_agg, 1)
                if nodes:
                    pe.wait_ge(s_ln, i - T0)
                    for t in range(NPT):
                        last = pe.matmul(ps_agg[H:P, t * P:(t + 1) * P], hs[:, 1 - k, t, :], ident[:, :],
                                         start=True, stop=True)
                    last.then_inc(s_hT, 1)
                if opens:
                    pe.wait_ge(s_h0, i + 1)
                    pe.matmul(ps_l1[:, 0:n], wl1[:, :], h0[:, 0:n], start=True, stop=True).then_inc(s_l1, 1)

            attrs_turned(0, 0, 16)
            edge_iter(0, 0, True, False, False, 16, False)
            edge_iter(1, 1, True, True, False, 32, False)
            for i in (2, 3, 4):
                edge_iter(i, i % 2, True, True, True, 16 * ((i + 1) // 2 + 1), False)
            with pe.Fori(2, PARTS // 2 + 2) as n:
                edge_iter(n * 2 + 1, 1, True, True, True, n * 16 + 32, True)
                edge_iter(n * 2 + 2, 0, True, True, True, n * 16 + 32, True)
            pe.wait_ge(s_bad, 1)
            pe.wait_ge(s_hTc, PARTS)
            pe.matmul(ps_agg[H:H + 1, 0:1], bad[:, 2:3], ones[:, :], start=True, stop=True).then_inc(s_flagp, 1)
            with pe.Fori(PARTS // 2 + 2, GROUPS // 2 - 2) as n:
                edge_iter(n * 2 + 1, 1, True, True, True, n * 16 + 32, False)
                edge_iter(n * 2 + 2, 0, True, True, True, n * 16 + 32, False)
            n = GROUPS // 2
            pe.wait_ge(s_flag, 1)
            f = pe.value_load(flag[0:1, 0:1], min_val=0, max_val=P)
            edge_iter(GROUPS - 3, 1, True, True, True, n * 16, False)
            edge_iter(GROUPS - 2, 0, True, True, True, n * 16 - 16 + 16 * TAILC, False)
            edge_iter(GROUPS - 1, 1, True, True, True, None, False)
            edge_iter(GROUPS, 0, False, True, True, None, False)
            edge_iter(GROUPS + 1, 1, False, False, True, None, False)

            with pe.If(f > 0):
                with pe.Fori(1, E // SLOW + 1) as v:
                    pe.wait_ge(s_fz, 1)
                    pe.wait_ge(s_frow, v)
                    pe.transpose(ps_ta[:, 0:SLOW], slow_rows[:, :, :].rearrange("p k d -> p (k d)"),
                                 ident[0:SLOW, 0:SLOW]).then_inc(s_fT, 1)
                    pe.wait_ge(s_fz, 1)
                    pe.wait_ge(s_fx, v)
                    pe.matmul(ps_l0[0:H, 0:SLOW], wl0[:, :], xT[:, 0:SLOW], start=True, stop=True).then_inc(s_fl[0], 1)
                    for k, (ps, w, h) in enumerate(((ps_l1, wl1, h0), (ps_l2, wl2, h1))):
                        pe.wait_ge(s_fz, 1)
                        pe.wait_ge(s_fh[k], v)
                        pe.matmul(ps[0:H, 0:SLOW], w[0:H, 0:H], h[0:H, 0:SLOW], start=True, stop=True).then_inc(s_fl[k + 1], 1)
                    pe.wait_ge(s_fz, 1)
                    pe.wait_ge(s_fh[2], v)
                    pe.transpose(ps_t2[0][0:SLOW, 0:H], h2[0:H, 0:SLOW], ident[0:H, 0:H]).then_inc(s_fU, 1)
                    pe.wait_ge(s_fz, 1)
                    pe.wait_ge(s_frd, v)
                    pe.matmul(ps_tb[0:H, 0:SLOW], slow_cen[:, :], slow_diag[:, :], start=True, stop=True).then_inc(s_fm, 1)

            pe.wait_ge(s_sums, 1)
            hv = h2[:, :].rearrange("d (p t) -> d t p", t=HALF)
            for q in range(PAIRS + 1):
                if q < PAIRS:
                    c0 = 2 * q * NODES
                    if q:
                        pe.wait_ge(s_nh0, q)
                    for h in range(2):
                        last = pe.matmul(ps_l0[h * H:(h + 1) * H, :], wn0[:, :],
                                         node_in[:, c0 + h * NODES:c0 + (h + 1) * NODES], start=True, stop=True)
                    last.then_inc(s_n0, 1)
                if q:
                    pe.wait_ge(s_nh1, q)
                    if q > 1:
                        pe.wait_ge(s_nh2, q - 1)
                    pe.matmul(ps_l2[:, :], wn2[:, :], h1[:, :], start=True, stop=True).then_inc(s_n2, 1)
                if q < PAIRS:
                    pe.wait_ge(s_nh0, q + 1)
                    if q:
                        pe.wait_ge(s_nh1, q)
                    pe.matmul(ps_l1[:, :], wn1[:, :], h0[:, :], start=True, stop=True).then_inc(s_n1, 1)
                if q:
                    pe.wait_ge(s_nh2, q)
                    if q > 1:
                        pe.wait_ge(s_nvar, q - 1)
                    for t in range(HALF):
                        last = pe.transpose(ps_t2[0][:, t * P:(t + 1) * P], hv[:, t, :], ident[:, :])
                    last.then_inc(s_nt, 1)
                    if q > 2:
                        pe.wait_ge(s_nscaled, q - 2)
                    for t in range(HALF):
                        last = pe.matmul((ps_ta, ps_tb)[(q - 1) % 2][:, t * P:(t + 1) * P], hv[:, t, :], wno[:, :],
                                         start=True, stop=True)
                    last.then_inc(s_no, 1)


def pack_weights(wt):
    import numpy as _np
    at, cols = weight_columns()
    packed = _np.zeros((128, cols), _np.float32)

    def place(name, row, a, col=0):
        a = a.reshape(a.shape[0], -1)
        c = at[name][0] + col
        packed[row:row + a.shape[0], c:c + a.shape[1]] = a

    w1_0, w2_0 = wt["w1_0"], wt["w2_0"]
    for lo in (0, 64):
        for name, a in (("l0h", w1_0[:64]), ("l0e", w1_0[64:]), ("l1", wt["w1_1"]), ("l2", wt["w1_2"]),
                        ("n1", wt["w2_1"]), ("n2", wt["w2_2"])):
            place(name, lo, a, lo)
        for k in range(3):
            place("bias1", lo, wt[f"b1_{k}"], k)
            place("bias2", lo, wt[f"b2_{k}"], k)
    place("l0", 0, w1_0)
    place("n0", 64, w2_0[:64])
    place("w2a", 0, w2_0[64:128])
    place("w2u", 0, w2_0[128:])
    place("w1o", 0, wt["w1_o"])
    place("w2o", 0, wt["w2_o"])
    for k, a in enumerate((wt["g1"], wt["be1"], wt["b1_o"], wt["u"][0], wt["g2"], wt["be2"])):
        place("col", 0, a, k)
    place("bo", 0, wt["b2_o"].reshape(1, 64))
    return packed


def kernel(**inputs):
    import numpy as _np
    import concourse.bacc as _bacc
    from concourse import mybir as _mybir
    from concourse.bass_utils import run_bass_kernel_spmd as _run

    nc = _bacc.Bacc("TRN2", target_bir_lowering=False, num_devices=1)
    arrays, args = {}, []
    given = {"x": inputs["x"], "src": inputs["src"], "dst": inputs["dst"], "edge_attr": inputs["edge_attr_64"],
             "weights": pack_weights({n[7:]: _np.asarray(a) for n, a in inputs.items() if n.startswith("L0_gnn_")})}
    for name, a in given.items():
        a = _np.ascontiguousarray(a)
        arrays[f"in_{name}_dram"] = a
        args.append(nc.dram_tensor(f"in_{name}_dram", a.shape, _mybir.dt.from_np(a.dtype), kind="ExternalInput").ap())
    shape = tuple(inputs['x'].shape)
    out = nc.dram_tensor("out_0_dram", shape, _mybir.dt.float32, kind="ExternalOutput").ap()
    gnn_layer(nc, *args, out)
    r = _run(nc, [arrays], core_ids=[0])
    return r.results[0]["out_0_dram"]
```
